# Optimizing a Trainium2 kernel written in Bass

```python
import numpy as np
import jax
import jax.numpy as jnp

def _softmax(x, axis=-1):
    return jax.nn.softmax(x, axis=axis)

def _gelu(x):
    return jax.nn.gelu(x, approximate=True)

def _silu(x):
    return jax.nn.silu(x)

def _sigmoid(x):
    return jax.nn.sigmoid(x)

def _layernorm(x, axis=-1, eps=1e-05):
    m = jnp.mean(x, axis=axis, keepdims=True)
    v = jnp.var(x, axis=axis, keepdims=True)
    return (x - m) / jnp.sqrt(v + eps)

def _scatter_add(tgt, idx, src, axis=0):
    return tgt.at[idx].add(src)

def _segment_sum(src, seg, n):
    return jax.ops.segment_sum(src, seg, n)
kernel_name = 'mk_sandwich_d1_jaxref_r8_e66c07'

def setup_inputs(seed: int=0):
    np.random.seed(seed)
    _w = jnp.asarray

    def _L0_attn_setup():
        import math
        import jax, jax.numpy as jnp
        import numpy as np
        DIM = 128
        HID = 256
        QK = 128
        G = 32
        B, N = (4, 512)
        NUM_BUCKETS = 32
        MAX_DIST = 128

        def _rel_pos_bias(rel_emb, g, scale):
            pos = jnp.arange(g)
            rel = pos[None, :] - pos[:, None]
            n = -rel
            nb = NUM_BUCKETS // 2
            ret = (n < 0).astype(jnp.int32) * nb
            n = jnp.abs(n)
            max_exact = nb // 2
            is_small = n < max_exact
            val_large = max_exact + (jnp.log(jnp.maximum(n, 1).astype(jnp.float32) / max_exact) / math.log(MAX_DIST / max_exact) * (nb - max_exact)).astype(jnp.int32)
            val_large = jnp.minimum(val_large, nb - 1)
            bucket = ret + jnp.where(is_small, n, val_large)
            return rel_emb[bucket, 0] * scale

        def _layernorm(x, g, b, eps=1e-05):
            mu = jnp.mean(x, axis=-1, keepdims=True)
            var = jnp.mean((x - mu) ** 2, axis=-1, keepdims=True)
            return (x - mu) * jax.lax.rsqrt(var + eps) * g + b
        key = jax.random.key(seed)
        ks = jax.random.split(key, 8)
        return {'x': jax.random.normal(ks[0], (B, N, DIM), dtype=jnp.float32), 'ln_g': jnp.ones((DIM,), jnp.float32), 'ln_b': jnp.zeros((DIM,), jnp.float32), 'W_h': jax.random.normal(ks[1], (DIM, 2 * HID), jnp.float32) * 0.02, 'b_h': jnp.zeros((2 * HID,), jnp.float32), 'W_qk': jax.random.normal(ks[2], (DIM, QK), jnp.float32) * 0.02, 'b_qk': jnp.zeros((QK,), jnp.float32), 'os_gamma': jax.random.normal(ks[3], (4, QK), jnp.float32) * 0.02, 'os_beta': jnp.zeros((4, QK), jnp.float32), 'rel_emb': jax.random.normal(ks[4], (NUM_BUCKETS, 1), jnp.float32) * 0.02, 'W_out': jax.random.normal(ks[5], (HID, DIM), jnp.float32) * 0.02, 'b_out': jnp.zeros((DIM,), jnp.float32)}
    _L0_attn_in = _L0_attn_setup()

    def _L0_ffn_setup():
        import jax, jax.numpy as jnp
        import numpy as np
        D_IN, D_HID = (128, 512)

        def _ternary(key, shape):
            return jax.random.randint(key, shape, -1, 2).astype(jnp.float32)

        def _tlin(x, w, s):
            return jnp.einsum('bsi,oi->bso', x, w) * s
        key = jax.random.key(seed)
        ks = jax.random.split(key, 12)
        inv = lambda fan: 1.0 / np.sqrt(fan).astype(np.float32)
        return {'x': jax.random.normal(ks[0], (4, 256, D_IN), dtype=jnp.float32), 'w1_w': _ternary(ks[1], (D_HID, D_IN)), 'w1_s': jax.random.uniform(ks[2], (D_HID,), dtype=jnp.float32) * inv(D_IN), 'w2_w': _ternary(ks[3], (D_HID, D_IN)), 'w2_s': jax.random.uniform(ks[4], (D_HID,), dtype=jnp.float32) * inv(D_IN), 'h1_w': _ternary(ks[5], (D_HID, D_HID)), 'h1_s': jax.random.uniform(ks[6], (D_HID,), dtype=jnp.float32) * inv(D_HID), 'h2_w': _ternary(ks[7], (D_HID, D_HID)), 'h2_s': jax.random.uniform(ks[8], (D_HID,), dtype=jnp.float32) * inv(D_HID), 'w3_w': _ternary(ks[9], (D_IN, D_HID)), 'w3_s': jax.random.uniform(ks[10], (D_IN,), dtype=jnp.float32) * inv(D_HID)}
    _L0_ffn_in = _L0_ffn_setup()
    _d = {'L0_attn_x': _L0_attn_in['x'], 'L0_attn_ln_g': _L0_attn_in['ln_g'], 'L0_attn_ln_b': _L0_attn_in['ln_b'], 'L0_attn_W_h': _L0_attn_in['W_h'], 'L0_attn_b_h': _L0_attn_in['b_h'], 'L0_attn_W_qk': _L0_attn_in['W_qk'], 'L0_attn_b_qk': _L0_attn_in['b_qk'], 'L0_attn_os_gamma': _L0_attn_in['os_gamma'], 'L0_attn_os_beta': _L0_attn_in['os_beta'], 'L0_attn_rel_emb': _L0_attn_in['rel_emb'], 'L0_attn_W_out': _L0_attn_in['W_out'], 'L0_attn_b_out': _L0_attn_in['b_out'], 'L0_ffn_w1_w': _L0_ffn_in['w1_w'], 'L0_ffn_w1_s': _L0_ffn_in['w1_s'], 'L0_ffn_w2_w': _L0_ffn_in['w2_w'], 'L0_ffn_w2_s': _L0_ffn_in['w2_s'], 'L0_ffn_h1_w': _L0_ffn_in['h1_w'], 'L0_ffn_h1_s': _L0_ffn_in['h1_s'], 'L0_ffn_h2_w': _L0_ffn_in['h2_w'], 'L0_ffn_h2_s': _L0_ffn_in['h2_s'], 'L0_ffn_w3_w': _L0_ffn_in['w3_w'], 'L0_ffn_w3_s': _L0_ffn_in['w3_s']}
    _x0 = _d['L0_attn_x']
    _d['L0_attn_x'] = jax.random.normal(jax.random.fold_in(jax.random.key(seed), 1), (16, 256, 128), dtype=_x0.dtype)
    del _x0
    return _d

def reference(L0_attn_x, L0_attn_ln_g, L0_attn_ln_b, L0_attn_W_h, L0_attn_b_h, L0_attn_W_qk, L0_attn_b_qk, L0_attn_os_gamma, L0_attn_os_beta, L0_attn_rel_emb, L0_attn_W_out, L0_attn_b_out, L0_ffn_w1_w, L0_ffn_w1_s, L0_ffn_w2_w, L0_ffn_w2_s, L0_ffn_h1_w, L0_ffn_h1_s, L0_ffn_h2_w, L0_ffn_h2_s, L0_ffn_w3_w, L0_ffn_w3_s):

    def _L0_attn_ref(x, ln_g, ln_b, W_h, b_h, W_qk, b_qk, os_gamma, os_beta, rel_emb, W_out, b_out):
        import math
        import jax, jax.numpy as jnp
        import numpy as np
        DIM = 128
        HID = 256
        QK = 128
        G = 32
        B, N = (4, 512)
        NUM_BUCKETS = 32
        MAX_DIST = 128

        def _rel_pos_bias(rel_emb, g, scale):
            pos = jnp.arange(g)
            rel = pos[None, :] - pos[:, None]
            n = -rel
            nb = NUM_BUCKETS // 2
            ret = (n < 0).astype(jnp.int32) * nb
            n = jnp.abs(n)
            max_exact = nb // 2
            is_small = n < max_exact
            val_large = max_exact + (jnp.log(jnp.maximum(n, 1).astype(jnp.float32) / max_exact) / math.log(MAX_DIST / max_exact) * (nb - max_exact)).astype(jnp.int32)
            val_large = jnp.minimum(val_large, nb - 1)
            bucket = ret + jnp.where(is_small, n, val_large)
            return rel_emb[bucket, 0] * scale

        def _layernorm(x, g, b, eps=1e-05):
            mu = jnp.mean(x, axis=-1, keepdims=True)
            var = jnp.mean((x - mu) ** 2, axis=-1, keepdims=True)
            return (x - mu) * jax.lax.rsqrt(var + eps) * g + b
        b, n = (x.shape[0], x.shape[1])
        ng = n // G
        normed = _layernorm(x, ln_g, ln_b)
        hid = jax.nn.silu(normed @ W_h + b_h)
        v, gate = (hid[..., :HID], hid[..., HID:])
        qk = jax.nn.silu(normed @ W_qk + b_qk)
        heads = qk[..., None, :] * os_gamma + os_beta
        quad_q, lin_q, quad_k, lin_k = [heads[..., h, :] for h in range(4)]

        def grp(t):
            return t.reshape(b, ng, G, t.shape[-1])
        quad_q, quad_k, lin_q, lin_k, vg = map(grp, (quad_q, quad_k, lin_q, lin_k, v))
        sim = jnp.einsum('bgid,bgjd->bgij', quad_q, quad_k) / G
        sim = sim + _rel_pos_bias(rel_emb, G, QK ** 0.5)
        attn = jax.nn.relu(sim) ** 2
        quad_out = jnp.einsum('bgij,bgje->bgie', attn, vg)
        lin_kv = jnp.einsum('bgnd,bgne->bde', lin_k, vg) / n
        lin_out = jnp.einsum('bde,bgnd->bgne', lin_kv, lin_q)
        out = (quad_out + lin_out).reshape(b, n, HID)
        out = gate * out
        return out @ W_out + b_out + x

    def _L0_ffn_ref(x, w1_w, w1_s, w2_w, w2_s, h1_w, h1_s, h2_w, h2_s, w3_w, w3_s):
        import jax, jax.numpy as jnp
        import numpy as np
        D_IN, D_HID = (128, 512)

        def _ternary(key, shape):
            return jax.random.randint(key, shape, -1, 2).astype(jnp.float32)

        def _tlin(x, w, s):
            return jnp.einsum('bsi,oi->bso', x, w) * s
        h = jax.nn.silu(_tlin(x, w1_w, w1_s)) * _tlin(x, w2_w, w2_s)
        h = jax.nn.gelu(_tlin(h, h1_w, h1_s), approximate=False)
        h = jax.nn.gelu(_tlin(h, h2_w, h2_s), approximate=False)
        return _tlin(h, w3_w, w3_s)
    x = L0_attn_x
    x = x + _layernorm(_L0_attn_ref(_layernorm(x, axis=-1), L0_attn_ln_g, L0_attn_ln_b, L0_attn_W_h, L0_attn_b_h, L0_attn_W_qk, L0_attn_b_qk, L0_attn_os_gamma, L0_attn_os_beta, L0_attn_rel_emb, L0_attn_W_out, L0_attn_b_out), axis=-1)
    x = x + _layernorm(_L0_ffn_ref(_layernorm(x, axis=-1), L0_ffn_w1_w, L0_ffn_w1_s, L0_ffn_w2_w, L0_ffn_w2_s, L0_ffn_h1_w, L0_ffn_h1_s, L0_ffn_h2_w, L0_ffn_h2_s, L0_ffn_w3_w, L0_ffn_w3_s), axis=-1)
    return x

_drawn_inputs = setup_inputs


def setup_inputs(seed=0):
    import zlib

    import numpy as np

    out = dict(_drawn_inputs(seed))
    spreads = {'L0_attn_ln_g': (1.0, 0.6),
     'L0_attn_ln_b': (0.0, 0.8),
     'L0_attn_b_h': (0.0, 0.8),
     'L0_attn_b_qk': (0.0, 2.0),
     'L0_attn_os_beta': (0.0, 0.8),
     'L0_attn_b_out': (0.0, 0.8)}
    factors = {'L0_attn_W_h': 8.0,
     'L0_attn_W_qk': 8.0,
     'L0_attn_os_gamma': 8.0,
     'L0_attn_rel_emb': 8.0,
     'L0_attn_W_out': 8.0}
    for name, (base, spread) in spreads.items():
        noise = np.random.default_rng([zlib.crc32(name.encode()), seed]).standard_normal(out[name].shape)
        drawn = base * np.exp(spread * noise) if base else spread * noise
        out[name] = jnp.asarray(drawn.astype(out[name].dtype))
    for name, factor in factors.items():
        out[name] = (out[name] * factor).astype(out[name].dtype)
    return out
```

```python
from contextlib import ExitStack

import numpy as np

import concourse.bass as bass
from concourse import mybir

P = 128
DIM = 128
HID = 256
FFN = 512
TOKENS = 4096
ROW = 256
GROUP = 32
CHUNK = 512
CHUNKS = TOKENS // CHUNK
TILES = CHUNK // P
ROWS = CHUNK // ROW
KF = FFN // P
KH = HID // P
BUCKETS = 32
MAX_DIST = 128
EPS = 1e-5
MASKED = -1e38

W1, W2, H1, H2, W3 = 0, FFN, 2 * FFN, 2 * FFN + KF * FFN, 2 * FFN + 2 * KF * FFN
FFN_COLS = W3 + KF * DIM
FFN_PIECES = [(W1, H1), (H1, H2), (H2, FFN_COLS)]
WV, WG, WQK, WOUT = 0, HID, 2 * HID, 2 * HID + DIM
ATT_COLS = WOUT + KH * DIM
C_LNG, C_LNB, C_BG, C_BQK, C_GAMMA, C_BETA = 0, 1, 2, 4, 5, 9
C_S1, C_S2, C_SH1, C_SH2, C_S3 = 13, 17, 21, 25, 29
VEC_COLS = 30
QUAD_Q, LIN_Q, QUAD_K, LIN_K = range(4)

F32 = mybir.dt.float32
F32R = mybir.dt.float32r
I32 = mybir.dt.int32
ALU = mybir.AluOpType
ACT = mybir.ActivationFunctionType
AX_X = mybir.AxisListType.X


def build(nc, x, att_w, ffn_w, vectors, bias_v, b_out, rel_emb, one_hot, own_keys, identity, out):
    ctx = ExitStack()
    with ctx:
        def sb(name, shape, dt=F32):
            return ctx.enter_context(nc.sbuf_tensor(name, shape, dt))

        def sem(name):
            return ctx.enter_context(nc.semaphore(name))

        att = sb("att", [P, ATT_COLS])
        att_hi = sb("att_hi", [P, WOUT], F32R)
        att_lo = sb("att_lo", [P, WOUT], F32R)
        ffn = sb("ffn", [P, FFN_COLS])
        ffn_hi = sb("ffn_hi", [P, FFN_COLS], F32R)
        ffn_lo = sb("ffn_lo", [P, FFN_COLS], F32R)
        vec = sb("vec", [P, VEC_COLS])
        ident = sb("ident", [P, P])
        hot = sb("hot", [BUCKETS, GROUP * GROUP])
        own_key = sb("own_key", [P, GROUP])
        rel = sb("rel", [BUCKETS, 1])
        rel_wide = sb("rel_wide", [BUCKETS, P])
        rel_group = sb("rel_group", [P, GROUP])
        rel_bias = sb("rel_bias", [P, P])
        bout = sb("bout", [P, DIM])
        BR = GROUP + 1
        lnb_pair = sb("lnb_pair", [P, BR])
        bias_raw = sb("bias_raw", [BR, HID])
        bias_sum = sb("bias_sum", [BR, HID])
        bias_rnd = sb("bias_rnd", [BR, HID], F32R)
        bias_rows = sb("bias_rows", [BR, HID], F32R)
        ones_r = sb("ones_r", [BR, P], F32R)
        bias_gqk = sb("bias_gqk", [P, KH + 1])
        ones = sb("ones", [P, 1])
        minus_half = sb("minus_half", [P, 2 * TILES])
        lo_sums = sb("lo_sums", [P, len(FFN_PIECES)])
        lo_total = sb("lo_total", [1, 1])
        lo_flag = sb("lo_flag", [1, 1], I32)

        x_in = sb("x_in", [P, TILES, DIM])
        x_res = sb("x_res", [P, TILES, DIM])
        x_norm = sb("x_norm", [P, TILES, DIM])
        x_norm_b = sb("x_norm_b", [P, TILES, DIM])
        x_hat = sb("x_hat", [P, TILES, DIM])
        xt_hi = sb("xt_hi", [P, CHUNK], F32R)
        xt_lo = sb("xt_lo", [P, CHUNK], F32R)
        qk_t = sb("qk_t", [P, CHUNK])
        v_tok = sb("v_tok", [P, TILES, HID])
        gate_t = sb("gate_t", [P, KH, CHUNK])
        head_t = sb("head_t", [P, 4, CHUNK])
        lin_k = sb("lin_k", [P, TILES, DIM])
        lin_kv = sb("lin_kv", [P, ROWS, HID])
        sim_b = sb("sim_b", [P, TILES, P])
        attn = sb("attn", [P, TILES, P])
        gated_t = sb("gated_t", [P, KH, CHUNK])
        y_att = sb("y_att", [P, TILES, DIM])
        y_hat = sb("y_hat", [P, TILES, DIM])
        x1 = sb("x1", [P, TILES, DIM])
        x1_hat = sb("x1_hat", [P, TILES, DIM])
        x1_res = sb("x1_res", [P, TILES, DIM])
        x1t_hi = sb("x1t_hi", [P, CHUNK], F32R)
        x1t_lo = sb("x1t_lo", [P, CHUNK], F32R)
        silu_h0 = sb("silu_h0", [P, 2 * KF, CHUNK])
        silu_t, h0 = silu_h0[:, 0:KF, :], silu_h0[:, KF:2 * KF, :]
        rel_picked = silu_h0[:, 0:2, :].rearrange("p m n -> p (m n)").rearrange(
            "p (q k) -> p q k", k=GROUP)
        h0_hi = sb("h0_hi", [P, KF, CHUNK], F32R)
        h0_lo = sb("h0_lo", [P, KF, CHUNK], F32R)
        gelu_t = sb("gelu_t", [P, KF, CHUNK])
        att_g = gelu_t[:, 0:2, :].rearrange("p m n -> p (m n)")[:, 0:WOUT]
        g1_hi = sb("g1_hi", [P, KF, CHUNK], F32R)
        g1_lo = sb("g1_lo", [P, KF, CHUNK], F32R)
        g2_hi, g2_lo = h0_hi, h0_lo
        z_t = sb("z_t", [P, CHUNK])
        z_hat = sb("z_hat", [P, TILES, DIM])
        y_out = sb("y_out", [P, TILES, DIM])
        bn = {n: sb(f"bn_{n}", [P, TILES, 6]) for n in ("x", "att", "x1", "ffn")}
        mv = {n: sb(f"mv_{n}", [P, TILES, 2]) for n in ("x", "att", "x1", "ffn")}
        arg = {n: sb(f"arg_{n}", [P, 2 * TILES]) for n in ("x", "att", "x1", "ffn")}
        rstd = {n: sb(f"rstd_{n}", [P, 2 * TILES]) for n in ("x", "att", "x1", "ffn")}

        bank = [ctx.enter_context(nc.psum_tensor(f"bank{b}", [P, CHUNK], F32)) for b in range(8)]
        B_LAST, B_V, B_KV, B_GATE, B_SIM, B_TURN, B_TOK = 0, (1, 2), 5, (4, 5), 4, 6, 7

        vec_in, att_in, x_loaded, res_loaded = sem("vec_in"), sem("att_in"), sem("x_loaded"), sem("res_loaded")
        rel_in, ident_in, bout_in, bias_in = sem("rel_in"), sem("ident_in"), sem("bout_in"), sem("bias_in")
        ffn_in = [sem(f"ffn_in{p}") for p in range(len(FFN_PIECES))]
        out_free = sem("out_free")
        waits_passed = sem("waits_passed")
        consts_set, att_scaled, att_rounded, att_split = (
            sem("consts_set"), sem("att_scaled"), sem("att_rounded"), sem("att_split"))
        lnb_set, bias_ps, bias_added, bias_split = sem("lnb_set"), sem("bias_ps"), sem("bias_added"), sem("bias_split")
        rel_wide_set, rel_ps, rel_set, gqk_set = sem("rel_wide_set"), sem("rel_ps"), sem("rel_set"), sem("gqk_set")
        ffn_rounded, ffn_split, lo_summed, lo_ps, lo_total_set, lo_flag_set = (
            sem("ffn_rounded"), sem("ffn_split"), sem("lo_summed"), sem("lo_ps"), sem("lo_total_set"),
            sem("lo_flag_set"))
        bn_done = {n: sem(f"bn_done_{n}") for n in bn}
        mv_done = {n: sem(f"mv_done_{n}") for n in bn}
        arg_done = {n: sem(f"arg_done_{n}") for n in bn}
        rstd_done = {n: sem(f"rstd_done_{n}") for n in bn}
        x_normed, x_hat_set, norm_b_set = sem("x_normed"), sem("x_hat_set"), sem("norm_b_set")
        xt_ps, xt_hi_set, xt_lo_set = sem("xt_ps"), sem("xt_hi_set"), sem("xt_lo_set")
        qk_ps, v_ps, gate_ps = sem("qk_ps"), sem("v_ps"), sem("gate_ps")
        qk_set, v_set, gate_set = sem("qk_set"), sem("v_set"), sem("gate_set")
        lin_k_head, quad_heads, lin_q_head = sem("lin_k_head"), sem("quad_heads"), sem("lin_q_head")
        lin_k_ps, lin_k_set, kv_ps, kv_set = sem("lin_k_ps"), sem("lin_k_set"), sem("kv_ps"), sem("kv_set")
        sim_ps, sim_biased, attn_set = sem("sim_ps"), sem("sim_biased"), sem("attn_set")
        mix_ps, gated_set = sem("mix_ps"), sem("gated_set")
        proj_ps, y_att_set, y_hat_set, x1_set, x1_hat_set = (
            sem("proj_ps"), sem("y_att_set"), sem("y_hat_set"), sem("x1_set"), sem("x1_hat_set"))
        x1_kept, x1t_ps, x1t_hi_set, x1t_lo_set = (
            sem("x1_kept"), sem("x1t_ps"), sem("x1t_hi_set"), sem("x1t_lo_set"))
        w1_ps, w2_ps, silu_set = sem("w1_ps"), sem("w2_ps"), sem("silu_set")
        h0_set, h0_hi_set, h0_lo_set = sem("h0_set"), sem("h0_hi_set"), sem("h0_lo_set")
        h1_ps, gelu1_set, g1_hi_set, g1_lo_set = sem("h1_ps"), sem("gelu1_set"), sem("g1_hi_set"), sem("g1_lo_set")
        h2_ps, gelu2_set, g2_hi_set, g2_lo_set = sem("h2_ps"), sem("gelu2_set"), sem("g2_hi_set"), sem("g2_lo_set")
        w3_ps, z_set, z_tok_ps, z_hat_set, out_ready = (
            sem("w3_ps"), sem("z_set"), sem("z_tok_ps"), sem("z_hat_set"), sem("out_ready"))

        x_chunks = x.rearrange("(c t p) d -> c p t d", p=P, t=TILES)
        out_chunks = out.rearrange("(c t p) d -> c p t d", p=P, t=TILES)

        def col(c, n=1):
            return vec[:, c:c + n]

        def cols(t):
            return slice(t * P, (t + 1) * P)

        def flat(buffer):
            return buffer[:, :, :].rearrange("p t d -> p (t d)")

        def i_is_followed(i):
            return not (isinstance(i, int) and i == CHUNKS - 1)

        block = ctx.enter_context(nc.Block())

        @block.sync
        def _(sp):
            def load_x(i):
                if not (isinstance(i, int) and i == 0):
                    sp.wait_ge(x_hat_set, i)
                    sp.wait_ge(x_normed, i)
                sp.dma_start(x_in[:, :, :], x_chunks[i]).then_inc(x_loaded, 16)

            def load_residual(i):
                if not (isinstance(i, int) and i == 0):
                    sp.wait_ge(x1_set, i)
                sp.dma_start(x_res[:, :, :], x_chunks[i]).then_inc(res_loaded, 16)

            def store(f):
                sp.wait_ge(out_ready, f + 1)
                sp.dma_start(out_chunks[f], y_out[:, :, :]).then_inc(out_free, 16)

            sp.sem_inc(out_free, 16)
            load_x(0)
            sp.dma_start(vec[:, :], vectors).then_inc(vec_in, 16)
            sp.dma_start(att[:, :], att_w).then_inc(att_in, 16)
            sp.dma_start(ident[:, :], identity).then_inc(ident_in, 16)
            load_residual(0)
            for p, (a, b) in enumerate(FFN_PIECES):
                sp.dma_start(ffn[:, a:b], ffn_w[:, a:b]).then_inc(ffn_in[p], 16)
            load_x(1)
            load_residual(1)
            load_x(2)
            with sp.Fori(1, CHUNKS - 2) as i:
                load_residual(i + 1)
                store(i - 1)
                load_x(i + 2)
            load_residual(CHUNKS - 1)
            for f in range(CHUNKS - 3, CHUNKS):
                store(f)
            sp.wait_ge(out_free, 16 * (CHUNKS + 1))

        @block.tensor
        def _(pe):
            def turn_x_hat(i):
                pe.wait_ge(x_hat_set, i + 1)
                for t in range(TILES):
                    last = pe.transpose(bank[B_TURN][:, cols(t)], x_hat[:, t, :], ident[:, :])
                last.then_inc(xt_ps, 1)

            def project_qk(i, after_projection=True):
                pe.wait_ge(xt_hi_set, i + 1)
                pe.wait_ge(xt_lo_set, i + 1)
                if after_projection and not (isinstance(i, int) and i == 0):
                    pe.wait_ge(y_att_set, i)
                ps = bank[B_TOK][:, :]
                w = slice(WQK, WQK + DIM)
                pe.matmul(ps, att_hi[:, w], xt_hi[:, :], start=True, stop=False)
                pe.matmul(ps, att_hi[:, w], xt_lo[:, :], start=False, stop=False)
                pe.matmul(ps, att_lo[:, w], xt_hi[:, :], start=False, stop=True).then_inc(qk_ps, 1)

            def project_v(i):
                w = slice(WV, WV + HID)
                for t in range(TILES):
                    ps = bank[B_V[t // 2]][:, (t % 2) * HID:(t % 2 + 1) * HID]
                    pe.matmul(ps, xt_hi[:, cols(t)], att_hi[:, w], start=True, stop=False)
                    pe.matmul(ps, xt_lo[:, cols(t)], att_hi[:, w], start=False, stop=False)
                    pe.matmul(ps, xt_hi[:, cols(t)], att_lo[:, w], start=False, stop=False)
                    last = pe.matmul(ps, ones_r[:, :], bias_rows[:, :], start=False, stop=True)
                    if t % 2:
                        last.then_inc(v_ps, 1)

            def project_gate(i):
                for k in range(KH):
                    ps = bank[B_GATE[k]][:, :]
                    w = slice(WG + k * P, WG + (k + 1) * P)
                    pe.matmul(ps, att_hi[:, w], xt_hi[:, :], start=True, stop=False)
                    pe.matmul(ps, att_hi[:, w], xt_lo[:, :], start=False, stop=False)
                    pe.matmul(ps, att_lo[:, w], xt_hi[:, :], start=False, stop=True).then_inc(gate_ps, 1)

            def turn_keys(i):
                pe.wait_ge(lin_k_head, i + 1)
                for t in range(TILES):
                    last = pe.transpose(bank[B_TURN][:, cols(t)], head_t[:, LIN_K, cols(t)], ident[:, :])
                last.then_inc(lin_k_ps, 1)

            def similarities(i):
                pe.wait_ge(quad_heads, i + 1)
                pe.wait_ge(gate_set, KH * i + 1)
                for t in range(TILES):
                    last = pe.matmul(bank[B_SIM][:, cols(t)], head_t[:, QUAD_K, cols(t)],
                                     head_t[:, QUAD_Q, cols(t)], start=True, stop=True)
                last.then_inc(sim_ps, 1)

            def keys_values(i):
                pe.wait_ge(lin_k_set, i + 1)
                pe.wait_ge(v_set, 2 * i + 2)
                pe.wait_ge(gate_set, KH * i + KH)
                for r in range(ROWS):
                    for t in range(2):
                        last = pe.matmul(bank[B_KV][:, r * HID:(r + 1) * HID], lin_k[:, 2 * r + t, :],
                                         v_tok[:, 2 * r + t, :], start=(t == 0), stop=(t == 1))
                last.then_inc(kv_ps, 1)

            def mix(i):
                pe.wait_ge(kv_set, i + 1)
                pe.wait_ge(lin_q_head, i + 1)
                pe.wait_ge(attn_set, i + 1)
                for k in range(KH):
                    for r in range(ROWS):
                        pe.matmul(bank[B_GATE[k]][:, r * ROW:(r + 1) * ROW],
                                  lin_kv[:, r, k * P:(k + 1) * P],
                                  head_t[:, LIN_Q, r * ROW:(r + 1) * ROW], start=True, stop=False)
                        for t in (2 * r, 2 * r + 1):
                            last = pe.matmul(bank[B_GATE[k]][:, cols(t)], v_tok[:, t, k * P:(k + 1) * P],
                                             attn[:, t, :], start=False, stop=(t % 2 == 1))
                    last.then_inc(mix_ps, 1)

            def project_out(i):
                pe.wait_ge(gated_set, KH * i + KH)
                for t in range(TILES):
                    for k in range(KH):
                        last = pe.matmul(bank[B_TOK][:, cols(t)], gated_t[:, k, cols(t)],
                                         att[:, WOUT + k * DIM:WOUT + (k + 1) * DIM],
                                         start=(k == 0), stop=(k == KH - 1))
                last.then_inc(proj_ps, 1)

            def turn_x1_hat(i):
                pe.wait_ge(x1_hat_set, i + 1)
                pe.wait_ge(lin_k_set, i + 2 if i_is_followed(i) else CHUNKS)
                for t in range(TILES):
                    last = pe.transpose(bank[B_TURN][:, cols(t)], x1_hat[:, t, :], ident[:, :])
                last.then_inc(x1t_ps, 1)

            def weigh(ps, at, hi, lo, start, stop, with_lo):
                w = slice(at, at + P)
                pe.matmul(ps, ffn_hi[:, w], hi, start=start, stop=False)
                if with_lo:
                    pe.matmul(ps, ffn_lo[:, w], hi, start=False, stop=False)
                return pe.matmul(ps, ffn_hi[:, w], lo, start=False, stop=stop)

            def gated_layer(f, with_lo):
                pe.wait_ge(x1t_hi_set, f + 1)
                pe.wait_ge(x1t_lo_set, f + 1)
                for m in range(KF):
                    for at, b, done in ((W1, 2 * m % 4, w1_ps), (W2, 2 * m % 4 + 1, w2_ps)):
                        if m >= 2 and at == W1:
                            pe.wait_ge(silu_set, KF * f + m - 1)
                        if m >= 2 and at == W2:
                            pe.wait_ge(h0_set, KF * f + m - 1)
                        weigh(bank[b][:, :], at + m * P, x1t_hi[:, :], x1t_lo[:, :], True, True,
                              with_lo).then_inc(done, 1)

            def first_hidden_layer(f, with_lo):
                pe.wait_ge(silu_set, KF * f + KF - 1)
                hidden_layer(f, H1, h0_hi, h0_lo, h0_hi_set, h0_lo_set, h1_ps, with_lo)

            def hidden_layer(f, at, hi, lo, hi_set, lo_set, done, with_lo):
                for m in range(KF):
                    for k in range(KF):
                        if m == 0:
                            pe.wait_ge(hi_set, KF * f + k + 1)
                            pe.wait_ge(lo_set, KF * f + k + 1)
                        last = weigh(bank[m][:, :], at + k * FFN + m * P, hi[:, k, :], lo[:, k, :],
                                     k == 0, k == KF - 1, with_lo)
                    last.then_inc(done, 1)

            def last_layer(f, blocks, with_lo):
                for k in blocks:
                    pe.wait_ge(g2_hi_set, KF * f + k + 1)
                    pe.wait_ge(g2_lo_set, KF * f + k + 1)
                    last = weigh(bank[B_LAST][:, :], W3 + k * DIM, g2_hi[:, k, :], g2_lo[:, k, :],
                                 k == 0, k == KF - 1, with_lo)
                if KF - 1 in blocks:
                    last.then_inc(w3_ps, 1)

            def turn_z(f, i):
                pe.wait_ge(z_set, f + 1)
                if i is None:
                    pe.wait_ge(y_att_set, CHUNKS)
                else:
                    pe.wait_ge(qk_set, i + 2)
                for t in range(TILES):
                    last = pe.transpose(bank[B_TOK][:, cols(t)], z_t[:, cols(t)], ident[:, :])
                last.then_inc(z_tok_ps, 1)

            pe.wait_ge(att_in, 16)
            pe.wait_ge(lnb_set, 1)
            pe.matmul(bank[0][0:BR, 0:HID], lnb_pair[:, :], att[:, WV:WV + HID],
                      start=True, stop=True).then_inc(bias_ps, 1)
            for k in range(KH + 1):
                last = pe.matmul(bank[2][:, k:k + 1], att[:, WG + k * P:WG + (k + 1) * P],
                                 col(C_LNB), start=True, stop=True)
            last.then_inc(bias_ps, 1)

            pe.wait_ge(ident_in, 16)
            turn_x_hat(0)
            pe.wait_ge(att_split, 1)
            project_qk(0)
            pe.wait_ge(rel_in, 48)
            pe.wait_ge(rel_wide_set, 1)
            for n in range(2):
                last = pe.matmul(bank[3 + 3 * n][:, :], rel_wide[:, :], hot[:, n * CHUNK:(n + 1) * CHUNK],
                                 start=True, stop=True)
            last.then_inc(rel_ps, 1)
            pe.wait_ge(bias_split, 1)
            pe.wait_ge(gqk_set, 1)
            project_v(0)
            pe.wait_ge(rel_set, 1)
            turn_keys(0)
            project_gate(0)
            similarities(0)
            keys_values(0)
            mix(0)
            turn_x_hat(1)
            project_qk(1, after_projection=False)
            pe.wait_ge(qk_set, 2)
            project_out(0)
            project_v(1)
            turn_keys(1)
            project_gate(1)
            pe.wait_ge(lo_summed, len(FFN_PIECES))
            pe.matmul(bank[0][0:1, 0:len(FFN_PIECES)], ones[:, :], lo_sums[:, :],
                      start=True, stop=True).then_inc(lo_ps, 1)

            def steps(with_lo):
                def ffn_and_attention(i, ahead):
                    similarities(i)
                    turn_x1_hat(i - 1)
                    keys_values(i)
                    gated_layer(i - 1, with_lo)
                    mix(i)
                    first_hidden_layer(i - 1, with_lo)
                    project_out(i)
                    if ahead:
                        turn_x_hat(i + 1)
                    hidden_layer(i - 1, H2, g1_hi, g1_lo, g1_hi_set, g1_lo_set, h2_ps, with_lo)
                    last_layer(i - 1, range(KF - 1), with_lo)
                    if ahead:
                        project_qk(i + 1)
                    last_layer(i - 1, [KF - 1], with_lo)
                    if ahead:
                        project_v(i + 1)
                    turn_z(i - 1, i if ahead else None)
                    if ahead:
                        turn_keys(i + 1)
                        project_gate(i + 1)

                with pe.Fori(1, CHUNKS - 1) as i:
                    ffn_and_attention(i, True)
                ffn_and_attention(CHUNKS - 1, False)
                f = CHUNKS - 1
                turn_x1_hat(f)
                gated_layer(f, with_lo)
                first_hidden_layer(f, with_lo)
                hidden_layer(f, H2, g1_hi, g1_lo, g1_hi_set, g1_lo_set, h2_ps, with_lo)
                last_layer(f, range(KF), with_lo)
                turn_z(f, None)

            pe.wait_ge(lo_flag_set, 1)
            has_lo = pe.value_load(lo_flag[0:1, 0:1], min_val=0, max_val=1)
            with pe.If(has_lo):
                steps(True)
            with pe.Else():
                steps(False)

        @block.scalar
        def _(act):
            def activations_qk(i):
                act.wait_ge(qk_ps, i + 1)
                act.activation(qk_t[:, :], bank[B_TOK][:, :], ACT.Silu,
                               bias=bias_gqk[:, KH:KH + 1]).then_inc(qk_set, 1)

            def activations_v(i):
                for n in range(2):
                    act.wait_ge(v_ps, 2 * i + n + 1)
                    act.activation(v_tok[:, 2 * n:2 * n + 2, :].rearrange("p t d -> p (t d)"),
                                   bank[B_V[n]][:, :], ACT.Silu).then_inc(v_set, 1)

            def copy_keys(i):
                act.wait_ge(lin_k_ps, i + 1)
                act.copy(flat(lin_k), bank[B_TURN][:, :]).then_inc(lin_k_set, 1)

            def activations_gate(i):
                for k in range(KH):
                    act.wait_ge(gate_ps, KH * i + k + 1)
                    act.activation(gate_t[:, k, :], bank[B_GATE[k]][:, :], ACT.Silu,
                                   bias=bias_gqk[:, k:k + 1]).then_inc(gate_set, 1)

            def round_x_hat(i):
                act.wait_ge(xt_ps, i + 1)
                act.copy(xt_hi[:, :], bank[B_TURN][:, :]).then_inc(xt_hi_set, 1)

            def scale_kv(i):
                act.wait_ge(kv_ps, i + 1)
                act.mul(flat(lin_kv), bank[B_KV][:, :], 1.0 / ROW).then_inc(kv_set, 1)

            def round_ffn(p):
                a, b = FFN_PIECES[p]
                act.wait_ge(ffn_in[p], 16)
                act.copy(ffn_hi[:, a:b], ffn[:, a:b]).then_inc(ffn_rounded, 1)

            def sum_ffn_low(p):
                a, b = FFN_PIECES[p]
                act.wait_ge(ffn_split, p + 1)
                act.activation(ffn[:, a:b], ffn_lo[:, a:b].bitcast(F32), ACT.Abs,
                               accum_out=lo_sums[:, p:p + 1]).then_inc(lo_summed, 1)

            def round_x1_hat(i):
                act.wait_ge(x1t_ps, i + 1)
                act.copy(x1t_hi[:, :], bank[B_TURN][:, :]).then_inc(x1t_hi_set, 1)

            def silu_w1(f):
                for m in range(KF):
                    act.wait_ge(w1_ps, KF * f + m + 1)
                    act.activation(silu_t[:, m, :], bank[2 * m % 4][:, :], ACT.Silu,
                                   scale=col(C_S1 + m)).then_inc(silu_set, 1)

            def gelus(f, ps_done, scale, hi, gelu_set, hi_set):
                for m in range(KF):
                    act.wait_ge(ps_done, KF * f + m + 1)
                    act.activation(gelu_t[:, m, :], bank[m][:, :], ACT.Gelu,
                                   scale=col(scale + m)).then_inc(gelu_set, 1)
                    act.activation(hi[:, m, :], bank[m][:, :], ACT.Gelu,
                                   scale=col(scale + m)).then_inc(hi_set, 1)

            def scale_z(f):
                act.wait_ge(w3_ps, f + 1)
                act.mul(z_t[:, :], bank[B_LAST][:, :], col(C_S3)).then_inc(z_set, 1)

            act.dma_start(rel[:, :], rel_emb).then_inc(rel_in, 16)
            act.dma_start(hot[:, :], one_hot).then_inc(rel_in, 16)
            act.dma_start(own_key[:, :], own_keys).then_inc(rel_in, 16)
            act.wait_ge(consts_set, 1)
            for row in (0, GROUP):
                act.dma_start(bias_raw[row:row + 1, :], bias_v).then_inc(bias_in, 16)
            act.dma_start(bout[:, :], b_out.partition_broadcast(P)).then_inc(bout_in, 16)

            act.wait_ge(att_scaled, 1)
            act.copy(att_hi[:, :], att_g).then_inc(att_rounded, 1)
            round_x_hat(0)
            act.wait_ge(gqk_set, 1)
            activations_qk(0)
            activations_v(0)
            copy_keys(0)
            activations_gate(0)
            round_ffn(0)
            scale_kv(0)
            round_ffn(1)
            round_x_hat(1)
            round_ffn(2)
            activations_qk(1)
            sum_ffn_low(0)
            activations_v(1)
            copy_keys(1)
            activations_gate(1)
            sum_ffn_low(1)
            sum_ffn_low(2)

            def step(i, ahead):
                round_x1_hat(i - 1)
                scale_kv(i)
                silu_w1(i - 1)
                gelus(i - 1, h1_ps, C_SH1, g1_hi, gelu1_set, g1_hi_set)
                if ahead:
                    round_x_hat(i + 1)
                gelus(i - 1, h2_ps, C_SH2, g2_hi, gelu2_set, g2_hi_set)
                if ahead:
                    activations_qk(i + 1)
                scale_z(i - 1)
                if ahead:
                    activations_v(i + 1)
                    copy_keys(i + 1)
                    activations_gate(i + 1)

            with act.Fori(1, CHUNKS - 1) as i:
                step(i, True)
            step(CHUNKS - 1, False)
            f = CHUNKS - 1
            round_x1_hat(f)
            silu_w1(f)
            gelus(f, h1_ps, C_SH1, g1_hi, gelu1_set, g1_hi_set)
            gelus(f, h2_ps, C_SH2, g2_hi, gelu2_set, g2_hi_set)
            scale_z(f)

        @block.vector
        def _(dve):
            def statistics(name, i, tile_of):
                for t in range(TILES):
                    last = dve.bn_stats(bn[name][:, t, :], tile_of(t))
                last.then_inc(bn_done[name], 1)
                dve.wait_ge(bn_done[name], i + 1)
                dve.sem_inc(waits_passed, 1)
                for t in range(TILES):
                    last = dve.bn_aggr(mv[name][:, t, :], bn[name][:, t, :])
                last.then_inc(mv_done[name], 1)

            def normalize(name, to, tile_of, done, root=0):
                for t in range(TILES):
                    last = dve.tensor_scalar(to[:, t, :], tile_of(t), mv[name][:, t, 0:1],
                                             rstd[name][:, root + t:root + t + 1],
                                             ALU.subtract, ALU.mult)
                last.then_inc(done, 1)

            def of(buffer):
                return lambda t: buffer[:, t, :]

            def of_bank(b):
                return lambda t: bank[b][:, cols(t)]

            def x_statistics(i):
                dve.wait_ge(x_loaded, 16 * i + 16)
                statistics("x", i, of(x_in))

            def x_normalize(i):
                dve.wait_ge(rstd_done["x"], i + 1)
                if not (isinstance(i, int) and i == 0):
                    dve.wait_ge(norm_b_set, i)
                normalize("x", x_hat, of(x_in), x_hat_set, root=TILES)
                normalize("x", x_norm, of(x_in), x_normed)

            def low_x_hat(i):
                dve.wait_ge(xt_hi_set, i + 1)
                dve.tensor_tensor(xt_lo[:, :], bank[B_TURN][:, :], xt_hi[:, :].bitcast(F32),
                                  ALU.subtract).then_inc(xt_lo_set, 1)

            def heads(i):
                dve.wait_ge(qk_set, i + 1)
                for h, done in ((LIN_K, lin_k_head), (QUAD_K, None), (QUAD_Q, quad_heads)):
                    last = dve.tensor_scalar(head_t[:, h, :], qk_t[:, :], col(C_GAMMA + h),
                                             col(C_BETA + h), ALU.mult, ALU.add)
                    if done is not None:
                        last.then_inc(done, 1)

            def attention(i):
                dve.wait_ge(sim_ps, i + 1)
                dve.scalar_tensor_tensor(sim_b[:, :, :], bank[B_SIM][:, :].rearrange("p (t q) -> p t q", q=P),
                                         1.0 / GROUP, rel_bias[:, :].unsqueeze(1).broadcast_to([P, TILES, P]),
                                         ALU.mult, ALU.add).then_inc(sim_biased, 1)
                dve.wait_ge(sim_biased, i + 1)
                dve.scalar_tensor_tensor(flat(attn), flat(sim_b), 0.0, flat(sim_b),
                                         ALU.max, ALU.mult).then_inc(attn_set, 1)

            def gate_mix(i):
                for k in range(KH):
                    dve.wait_ge(mix_ps, KH * i + k + 1)
                    dve.tensor_tensor(gated_t[:, k, :], bank[B_GATE[k]][:, :], gate_t[:, k, :],
                                      ALU.mult).then_inc(gated_set, 1)

            def add_x_norm(i):
                dve.wait_ge(proj_ps, i + 1)
                dve.wait_ge(norm_b_set, i + 1)
                dve.tensor_tensor(flat(y_att), bank[B_TOK][:, :], flat(x_norm_b),
                                  ALU.add).then_inc(y_att_set, 1)
                dve.wait_ge(y_att_set, i + 1)
                statistics("att", i, of(y_att))

            def y_normalize(i):
                dve.wait_ge(rstd_done["att"], i + 1)
                normalize("att", y_hat, of(y_att), y_hat_set)

            def add_x(i):
                dve.wait_ge(y_hat_set, i + 1)
                dve.wait_ge(res_loaded, 16 * i + 16)
                if not (isinstance(i, int) and i == 0):
                    dve.wait_ge(x1_kept, i)
                dve.tensor_tensor(flat(x1), flat(y_hat), flat(x_res), ALU.add).then_inc(x1_set, 1)

            def x1_statistics(i):
                dve.wait_ge(x1_set, i + 1)
                statistics("x1", i, of(x1))

            def x1_normalize(i):
                dve.wait_ge(rstd_done["x1"], i + 1)
                normalize("x1", x1_hat, of(x1), x1_hat_set)

            def low_x1_hat(i):
                dve.wait_ge(x1t_hi_set, i + 1)
                dve.tensor_tensor(x1t_lo[:, :], bank[B_TURN][:, :], x1t_hi[:, :].bitcast(F32),
                                  ALU.subtract).then_inc(x1t_lo_set, 1)

            def gated_layer(f):
                def product(m):
                    dve.wait_ge(silu_set, KF * f + m + 1)
                    dve.wait_ge(w2_ps, KF * f + m + 1)
                    dve.scalar_tensor_tensor(h0[:, m, :], bank[2 * m % 4 + 1][:, :], col(C_S2 + m),
                                             silu_t[:, m, :], ALU.mult, ALU.mult).then_inc(h0_set, 1)

                def low(m):
                    dve.wait_ge(h0_hi_set, KF * f + m + 1)
                    dve.tensor_tensor(h0_lo[:, m, :], h0[:, m, :], h0_hi[:, m, :].bitcast(F32),
                                      ALU.subtract).then_inc(h0_lo_set, 1)

                product(0)
                for m in range(1, KF):
                    product(m)
                    low(m - 1)
                low(KF - 1)

            def low_gelu(f, m, hi, lo, hi_set, lo_set):
                dve.wait_ge(hi_set, KF * f + m + 1)
                dve.tensor_tensor(lo[:, m, :], gelu_t[:, m, :], hi[:, m, :].bitcast(F32),
                                  ALU.subtract).then_inc(lo_set, 1)

            def z_statistics(f):
                dve.wait_ge(z_tok_ps, f + 1)
                statistics("ffn", f, of_bank(B_TOK))

            def make_out(f):
                dve.wait_ge(rstd_done["ffn"], f + 1)
                normalize("ffn", z_hat, of_bank(B_TOK), z_hat_set)
                dve.wait_ge(z_hat_set, f + 1)
                dve.wait_ge(out_free, 16 * f + 16)
                dve.tensor_tensor(flat(y_out), flat(z_hat), flat(x1_res), ALU.add).then_inc(out_ready, 1)

            dve.memset(minus_half[:, :], -0.5)
            dve.memset(ones[:, :], 1.0)
            dve.memset(ones_r[:, :].bitcast(F32), 1.0)
            dve.memset(lnb_pair[:, :], 0.0)
            dve.memset(rel_bias[:, :], MASKED)
            dve.memset(bias_raw[:, :], 0.0).then_inc(consts_set, 1)
            x_statistics(0)
            dve.wait_ge(consts_set, 1)
            dve.wait_ge(vec_in, 16)
            for c in (0, GROUP):
                last = dve.tensor_copy(lnb_pair[:, c:c + 1], col(C_LNB))
            last.then_inc(lnb_set, 1)
            dve.wait_ge(rel_in, 48)
            dve.tensor_scalar(rel_wide[:, :], rel[:, 0:1].broadcast_to([BUCKETS, P]), 1.0, None,
                              ALU.mult).then_inc(rel_wide_set, 1)
            dve.wait_ge(att_in, 16)
            dve.tensor_scalar(att_g, att[:, 0:WOUT], col(C_LNG), None, ALU.mult).then_inc(att_scaled, 1)
            x_normalize(0)
            dve.wait_ge(att_rounded, 1)
            dve.tensor_tensor(att_lo[:, :], att_g, att_hi[:, :].bitcast(F32),
                              ALU.subtract).then_inc(att_split, 1)
            low_x_hat(0)
            dve.wait_ge(bias_ps, 2)
            dve.tensor_tensor(bias_gqk[:, :], bank[2][:, 0:KH + 1], col(C_BG, KH + 1), ALU.add).then_inc(gqk_set, 1)
            dve.wait_ge(bias_in, 32)
            dve.tensor_tensor(bias_sum[:, :], bank[0][0:BR, 0:HID], bias_raw[:, :], ALU.add).then_inc(bias_added, 1)
            dve.wait_ge(bias_added, 1)
            dve.tensor_copy(bias_rnd[:, :], bias_sum[:, :])
            dve.tensor_copy(bias_rows[:, :], bias_sum[:, :]).then_inc(bias_added, 1)
            dve.wait_ge(bias_added, 2)
            dve.tensor_tensor(bias_rows[GROUP:BR, :], bias_sum[GROUP:BR, :],
                              bias_rnd[GROUP:BR, :].bitcast(F32), ALU.subtract).then_inc(bias_split, 1)
            dve.wait_ge(rel_ps, 1)
            half = GROUP // 2
            for n in range(2):
                last = dve.tensor_tensor(rel_picked[:, n * half:(n + 1) * half, :],
                                         bank[3 + 3 * n][:, :].rearrange("p (q k) -> p q k", k=GROUP),
                                         own_key[:, :].unsqueeze(1).broadcast_to([P, half, GROUP]), ALU.mult)
            last.then_inc(rel_set, 1)
            dve.wait_ge(rel_set, 1)
            dve.reduce_sum(rel_group[:, :], rel_picked, AX_X).then_inc(rel_set, 1)
            dve.wait_ge(rel_set, 2)
            for g in range(P // GROUP):
                s = slice(g * GROUP, (g + 1) * GROUP)
                last = dve.tensor_scalar(rel_bias[s, s], rel_group[s, :], float(DIM) ** 0.5, None, ALU.mult)
            last.then_inc(rel_set, 1)
            x_statistics(1)
            heads(0)
            x_normalize(1)
            dve.wait_ge(rel_set, 3)
            attention(0)

            def low_ffn(p):
                a, b = FFN_PIECES[p]
                dve.wait_ge(ffn_rounded, p + 1)
                dve.tensor_tensor(ffn_lo[:, a:b], ffn[:, a:b], ffn_hi[:, a:b].bitcast(F32),
                                  ALU.subtract).then_inc(ffn_split, 1)

            low_ffn(0)
            gate_mix(0)
            low_x_hat(1)
            low_ffn(1)
            add_x_norm(0)
            y_normalize(0)
            add_x(0)
            x1_statistics(0)
            heads(1)
            x1_normalize(0)
            low_ffn(2)
            dve.wait_ge(lo_ps, 1)
            dve.reduce_sum(lo_total[:, :], bank[0][0:1, 0:len(FFN_PIECES)], AX_X).then_inc(lo_total_set, 1)
            dve.wait_ge(lo_total_set, 1)
            dve.tensor_scalar(lo_flag[:, :], lo_total[:, :], 0.0, None, ALU.is_gt).then_inc(lo_flag_set, 1)

            def step(i, ahead):
                f = i - 1
                low_x1_hat(f)
                attention(i)
                gated_layer(f)
                gate_mix(i)
                if ahead:
                    x_statistics(i + 1)
                low_gelu(f, 0, g1_hi, g1_lo, g1_hi_set, g1_lo_set)
                if ahead:
                    x_normalize(i + 1)
                for m in range(1, KF):
                    low_gelu(f, m, g1_hi, g1_lo, g1_hi_set, g1_lo_set)
                add_x_norm(i)
                if ahead:
                    low_x_hat(i + 1)
                low_gelu(f, 0, g2_hi, g2_lo, g2_hi_set, g2_lo_set)
                y_normalize(i)
                low_gelu(f, 1, g2_hi, g2_lo, g2_hi_set, g2_lo_set)
                add_x(i)
                low_gelu(f, 2, g2_hi, g2_lo, g2_hi_set, g2_lo_set)
                x1_statistics(i)
                low_gelu(f, 3, g2_hi, g2_lo, g2_hi_set, g2_lo_set)
                x1_normalize(i)
                if ahead:
                    heads(i + 1)
                z_statistics(f)
                make_out(f)

            with dve.Fori(1, CHUNKS - 1) as i:
                step(i, True)
            step(CHUNKS - 1, False)
            f = CHUNKS - 1
            low_x1_hat(f)
            gated_layer(f)
            for hi, lo, hi_set, lo_set in ((g1_hi, g1_lo, g1_hi_set, g1_lo_set),
                                           (g2_hi, g2_lo, g2_hi_set, g2_lo_set)):
                for m in range(KF):
                    low_gelu(f, m, hi, lo, hi_set, lo_set)
            z_statistics(f)
            make_out(f)

        @block.gpsimd
        def _(pool):
            def after(semaphore, value):
                pool.wait_ge(semaphore, value)
                pool.sem_inc(waits_passed, 1)

            def root(name, i, twice=False):
                after(mv_done[name], i + 1)
                last = pool.tensor_scalar(arg[name][:, 0:TILES], mv[name][:, :, 1], 1.0, EPS,
                                          ALU.mult, ALU.add)
                n = TILES
                if twice:
                    last = pool.tensor_scalar(arg[name][:, TILES:2 * TILES], mv[name][:, :, 1], 1.0 + EPS,
                                              EPS * EPS, ALU.mult, ALU.add)
                    n = 2 * TILES
                last.then_inc(arg_done[name], 1)
                pool.wait_ge(arg_done[name], i + 1)
                pool.tensor_tensor(rstd[name][:, 0:n], arg[name][:, 0:n], minus_half[:, 0:n],
                                   ALU.pow).then_inc(rstd_done[name], 1)

            def add_b_out(i):
                pool.wait_ge(x_normed, i + 1)
                if not (isinstance(i, int) and i == 0):
                    pool.wait_ge(y_att_set, i)
                pool.tensor_tensor(x_norm_b[:, :, :], x_norm[:, :, :],
                                   bout[:, :].unsqueeze(1).broadcast_to([P, TILES, DIM]),
                                   ALU.add).then_inc(norm_b_set, 1)

            def lin_q(i):
                after(qk_set, i + 1)
                pool.tensor_scalar(head_t[:, LIN_Q, :], qk_t[:, :], col(C_GAMMA + LIN_Q),
                                   col(C_BETA + LIN_Q), ALU.mult, ALU.add).then_inc(lin_q_head, 1)

            def round_h0(f):
                for m in range(KF):
                    after(h0_set, KF * f + m + 1)
                    pool.tensor_scalar(h0_hi[:, m, :], h0[:, m, :], 1.0, 0.0,
                                       ALU.mult, ALU.add).then_inc(h0_hi_set, 1)

            def keep_x1(f):
                after(x1_set, f + 1)
                pool.tensor_scalar(flat(x1_res), flat(x1), 1.0, 0.0, ALU.mult, ALU.add).then_inc(x1_kept, 1)

            pool.wait_ge(consts_set, 1)
            root("x", 0, twice=True)
            pool.wait_ge(bout_in, 16)
            add_b_out(0)
            pool.wait_ge(vec_in, 16)
            lin_q(0)
            root("x", 1, twice=True)
            root("att", 0)
            add_b_out(1)
            root("x1", 0)
            lin_q(1)

            def step(i, ahead):
                round_h0(i - 1)
                keep_x1(i - 1)
                if ahead:
                    root("x", i + 1, twice=True)
                root("att", i)
                if ahead:
                    add_b_out(i + 1)
                root("x1", i)
                if ahead:
                    lin_q(i + 1)
                root("ffn", i - 1)

            with pool.Fori(1, CHUNKS - 1) as i:
                step(i, True)
            step(CHUNKS - 1, False)
            round_h0(CHUNKS - 1)
            keep_x1(CHUNKS - 1)
            root("ffn", CHUNKS - 1)


def _bucket_table():
    pos = np.arange(GROUP)
    n = -(pos[None, :] - pos[:, None])
    nb = BUCKETS // 2
    ret = (n < 0).astype(np.int32) * nb
    n = np.abs(n)
    exact = nb // 2
    ratio = np.log(np.maximum(n, 1).astype(np.float32) / np.float32(exact)) / np.float32(np.log(MAX_DIST / exact))
    large = exact + (ratio * np.float32(nb - exact)).astype(np.int32)
    return ret + np.where(n < exact, n, np.minimum(large, nb - 1))


def _one_hot():
    hot = _bucket_table()[None, :, :] == np.arange(BUCKETS)[:, None, None]
    return hot.reshape(BUCKETS, -1).astype(np.float32)


def _blocks(w):
    o, n = w.shape
    return w.T.reshape(n // P, P, o).transpose(1, 0, 2).reshape(P, -1)


def _columns(v):
    return v.reshape(-1, P).T


def kernel(**inputs):
    import concourse.bacc as _bacc
    from concourse.bass_utils import run_bass_kernel_spmd as _run

    a = {k.removeprefix("L0_"): np.asarray(v) for k, v in inputs.items()}
    w_h, b_h = a["attn_W_h"], a["attn_b_h"]
    w_out = a["attn_W_out"].reshape(KH, P, DIM).transpose(1, 0, 2).reshape(P, -1)
    layout = {
        "x": a["attn_x"].reshape(TOKENS, DIM),
        "att_w": np.concatenate([w_h, a["attn_W_qk"], w_out], axis=1),
        "ffn_w": np.concatenate([_blocks(a[f"ffn_{n}_w"]) for n in ("w1", "w2", "h1", "h2", "w3")], axis=1),
        "vectors": np.concatenate(
            [_columns(v) for v in (a["attn_ln_g"], a["attn_ln_b"], b_h[HID:], a["attn_b_qk"],
                                   a["attn_os_gamma"], a["attn_os_beta"], a["ffn_w1_s"], a["ffn_w2_s"],
                                   a["ffn_h1_s"], a["ffn_h2_s"], a["ffn_w3_s"])], axis=1),
        "bias_v": b_h[:HID].reshape(1, HID),
        "b_out": a["attn_b_out"].reshape(1, DIM),
        "rel_emb": a["attn_rel_emb"],
        "one_hot": _one_hot(),
        "own_keys": np.tile(np.eye(GROUP, dtype=np.float32), (P // GROUP, 1)),
        "identity": np.eye(P, dtype=np.float32),
    }
    nc = _bacc.Bacc("TRN2", target_bir_lowering=False, num_devices=1)
    arrays, args = {}, []
    for name, v in layout.items():
        v = np.ascontiguousarray(v)
        arrays[f"in_{name}"] = v
        args.append(nc.dram_tensor(f"in_{name}", v.shape, F32, kind="ExternalInput").ap())
    out = nc.dram_tensor("out_x", (TOKENS, DIM), F32, kind="ExternalOutput").ap()
    build(nc, *args, out)
    r = _run(nc, [arrays], core_ids=[0])
    return r.results[0]["out_x"].reshape(inputs["L0_attn_x"].shape)
```

```python
from contextlib import ExitStack

import numpy as np

import concourse.bass as bass
from concourse import mybir

P = 128
DIM = 128
HID = 256
FFN = 512
TOKENS = 4096
ROW = 256
GROUP = 32
CHUNK = 512
CHUNKS = TOKENS // CHUNK
TILES = CHUNK // P
ROWS = CHUNK // ROW
KF = FFN // P
KH = HID // P
BUCKETS = 32
MAX_DIST = 128
EPS = 1e-5
WARM_UP = 9
MASKED = -1e38

W1, W2, H1, H2, W3 = 0, FFN, 2 * FFN, 2 * FFN + KF * FFN, 2 * FFN + 2 * KF * FFN
FFN_COLS = W3 + KF * DIM
FFN_PIECES = [(c, min(c + 2 * FFN, FFN_COLS)) for c in range(0, FFN_COLS, 2 * FFN)]
PIECES_OF_POOL = 4
WV, WG, WQK, WOUT = 0, HID, 2 * HID, 2 * HID + DIM
ATT_COLS = WOUT + KH * DIM
C_LNG, C_LNB, C_BG, C_BQK, C_GAMMA, C_BETA = 0, 1, 2, 4, 5, 9
C_S1, C_S2, C_SH1, C_SH2, C_S3 = 13, 17, 21, 25, 29
VEC_COLS = 30
QUAD_Q, LIN_Q, QUAD_K, LIN_K = range(4)

WHOLE = (slice(0, CHUNK), range(TILES), 0)
HALVES = [(CHUNKS - 1 + h, (slice(h * ROW, (h + 1) * ROW), range(2 * h, 2 * h + 2), 4 - 4 * h))
          for h in range(2)]

F32 = mybir.dt.float32
F32R = mybir.dt.float32r
I32 = mybir.dt.int32
ALU = mybir.AluOpType
ACT = mybir.ActivationFunctionType
AX_X = mybir.AxisListType.X


def build(nc, x, att_w, ffn_w, vectors, bias_v, b_out, rel_emb, one_hot, own_keys, identity, out):
    ctx = ExitStack()
    with ctx:
        def sb(name, shape, dt=F32):
            return ctx.enter_context(nc.sbuf_tensor(name, shape, dt))

        def sem(name):
            return ctx.enter_context(nc.semaphore(name))

        att = sb("att", [P, ATT_COLS])
        att_hi = sb("att_hi", [P, WOUT], F32R)
        att_lo = sb("att_lo", [P, WOUT], F32R)
        ffn = sb("ffn", [P, FFN_COLS])
        ffn_hi = sb("ffn_hi", [P, FFN_COLS], F32R)
        ffn_lo = sb("ffn_lo", [P, FFN_COLS], F32R)
        vec = sb("vec", [P, VEC_COLS])
        ident = sb("ident", [P, P])
        hot = sb("hot", [BUCKETS, GROUP * GROUP])
        own_key = sb("own_key", [P, GROUP])
        rel = sb("rel", [BUCKETS, 1])
        rel_wide = sb("rel_wide", [BUCKETS, P])
        rel_group = sb("rel_group", [P, GROUP])
        rel_bias = sb("rel_bias", [P, P])
        bout = sb("bout", [P, DIM])
        BR = GROUP + 1
        lnb_pair = sb("lnb_pair", [P, BR])
        bias_raw = sb("bias_raw", [BR, HID])
        bias_sum = sb("bias_sum", [BR, HID])
        bias_rnd = sb("bias_rnd", [BR, HID], F32R)
        bias_rows = sb("bias_rows", [BR, HID], F32R)
        ones_r = sb("ones_r", [BR, P], F32R)
        bias_gqk = sb("bias_gqk", [P, KH + 1])
        ones = sb("ones", [P, 1])
        unused = sb("unused", [P, 2])
        minus_half = sb("minus_half", [P, 2 * TILES])
        lo_sums = sb("lo_sums", [P, len(FFN_PIECES)])
        lo_total = sb("lo_total", [1, 1])
        lo_flag = sb("lo_flag", [1, 1], I32)

        x_in = sb("x_in", [P, TILES, DIM])
        x_res = sb("x_res", [P, TILES, DIM])
        x_norm = sb("x_norm", [P, TILES, DIM])
        x_norm_b = sb("x_norm_b", [P, TILES, DIM])
        x_hat = sb("x_hat", [P, TILES, DIM])
        xt_hi = sb("xt_hi", [P, CHUNK], F32R)
        xt_lo = sb("xt_lo", [P, CHUNK], F32R)
        qk_t = sb("qk_t", [P, CHUNK])
        v_tok = sb("v_tok", [P, TILES, HID])
        gate_t = sb("gate_t", [P, KH, CHUNK])
        head_t = sb("head_t", [P, 4, CHUNK])
        lin_k = sb("lin_k", [P, TILES, DIM])
        lin_kv = sb("lin_kv", [P, ROWS, HID])
        sim_b = sb("sim_b", [P, TILES, P])
        attn = sb("attn", [P, TILES, P])
        gated_t = sb("gated_t", [P, KH, CHUNK])
        y_att = sb("y_att", [P, TILES, DIM])
        y_hat = sb("y_hat", [P, TILES, DIM])
        x1 = sb("x1", [P, TILES, DIM])
        x1_hat = sb("x1_hat", [P, TILES, DIM])
        x1_res = sb("x1_res", [P, TILES, DIM])
        x1t_hi = sb("x1t_hi", [P, CHUNK], F32R)
        x1t_lo = sb("x1t_lo", [P, CHUNK], F32R)
        silu_h0 = sb("silu_h0", [P, 2 * KF, CHUNK])
        silu_t, h0 = silu_h0[:, 0:KF, :], silu_h0[:, KF:2 * KF, :]
        rel_picked = silu_h0[:, 0:2, :].rearrange("p m n -> p (m n)").rearrange(
            "p (q k) -> p q k", k=GROUP)
        h0_hi = sb("h0_hi", [P, KF, CHUNK], F32R)
        h0_lo = sb("h0_lo", [P, KF, CHUNK], F32R)
        gelu_t = sb("gelu_t", [P, KF, CHUNK])
        att_g = gelu_t[:, 0:2, :].rearrange("p m n -> p (m n)")[:, 0:WOUT]
        g1_hi = sb("g1_hi", [P, KF, CHUNK], F32R)
        g1_lo = sb("g1_lo", [P, KF, CHUNK], F32R)
        g2_hi, g2_lo = h0_hi, h0_lo
        z_t = sb("z_t", [P, CHUNK])
        z_hat = sb("z_hat", [P, TILES, DIM])
        y_out = sb("y_out", [P, TILES, DIM])
        NORMS = ("x0", "x", "att", "x1", "ffn")
        bn = {n: sb(f"bn_{n}", [P, TILES, 6]) for n in NORMS}
        mv = {n: sb(f"mv_{n}", [P, TILES, 2]) for n in NORMS}
        arg = {n: sb(f"arg_{n}", [P, 2 * TILES]) for n in NORMS}
        rstd = {n: sb(f"rstd_{n}", [P, 2 * TILES]) for n in NORMS}

        bank = [ctx.enter_context(nc.psum_tensor(f"bank{b}", [P, CHUNK], F32)) for b in range(8)]
        B_LAST, B_V, B_TURN1, B_KV, B_GATE, B_SIM, B_TURN, B_TOK = 0, (1, 2), 3, 5, (4, 5), 4, 6, 7
        B_REL, B_BIAS, B_UNUSED = (3, 0), 2, 1
        B_LAST_Z, B_Z = 3, 1

        vec_in, att_in, x_loaded, res_loaded = sem("vec_in"), sem("att_in"), sem("x_loaded"), sem("res_loaded")
        rel_in, ident_in, bout_in, bias_in = sem("rel_in"), sem("ident_in"), sem("bout_in"), sem("bias_in")
        ffn_in = [sem(f"ffn_in{p}") for p in range(len(FFN_PIECES))]
        out_w_in = sem("out_w_in")
        out_free = sem("out_free")
        waits_passed = sem("waits_passed")
        consts_set, att_scaled, att_rounded, att_split = (
            sem("consts_set"), sem("att_scaled"), sem("att_rounded"), sem("att_split"))
        lnb_set, bias_ps, bias_added, bias_split = sem("lnb_set"), sem("bias_ps"), sem("bias_added"), sem("bias_split")
        rel_wide_set, rel_ps, rel_set, gqk_set = sem("rel_wide_set"), sem("rel_ps"), sem("rel_set"), sem("gqk_set")
        ffn_rounded, lo_summed, lo_ps, lo_total_set, lo_flag_set = (
            sem("ffn_rounded"), sem("lo_summed"), sem("lo_ps"), sem("lo_total_set"), sem("lo_flag_set"))
        ffn_split = [sem(f"ffn_split{p}") for p in range(len(FFN_PIECES))]
        bn_done = {n: sem(f"bn_done_{n}") for n in bn}
        mv_done = {n: sem(f"mv_done_{n}") for n in bn}
        arg_done = {n: sem(f"arg_done_{n}") for n in bn}
        rstd_done = {n: sem(f"rstd_done_{n}") for n in bn}
        x_normed, x_hat_set, norm_b_set = sem("x_normed"), sem("x_hat_set"), sem("norm_b_set")
        xt_ps, xt_hi_set, xt_lo_set = sem("xt_ps"), sem("xt_hi_set"), sem("xt_lo_set")
        qk_ps, v_ps, gate_ps = sem("qk_ps"), sem("v_ps"), sem("gate_ps")
        qk_set, v_set, gate_set = sem("qk_set"), sem("v_set"), sem("gate_set")
        lin_k_head, quad_heads, lin_q_head = sem("lin_k_head"), sem("quad_heads"), sem("lin_q_head")
        lin_k_ps, lin_k_set, kv_ps, kv_set = sem("lin_k_ps"), sem("lin_k_set"), sem("kv_ps"), sem("kv_set")
        sim_ps, sim_biased, attn_set = sem("sim_ps"), sem("sim_biased"), sem("attn_set")
        mix_ps, gated_set = sem("mix_ps"), sem("gated_set")
        proj_ps, y_att_set, y_hat_set, x1_set, x1_hat_set = (
            sem("proj_ps"), sem("y_att_set"), sem("y_hat_set"), sem("x1_set"), sem("x1_hat_set"))
        x1_kept, x1t_ps, x1t_hi_set, x1t_lo_set = (
            sem("x1_kept"), sem("x1t_ps"), sem("x1t_hi_set"), sem("x1t_lo_set"))
        w1_ps, w2_ps, silu_set = sem("w1_ps"), sem("w2_ps"), sem("silu_set")
        h0_set, h0_hi_set, h0_lo_set = sem("h0_set"), sem("h0_hi_set"), sem("h0_lo_set")
        h1_ps, g1_hi_set, g1_lo_set = sem("h1_ps"), sem("g1_hi_set"), sem("g1_lo_set")
        h2_ps, g2_hi_set, g2_lo_set = sem("h2_ps"), sem("g2_hi_set"), sem("g2_lo_set")
        w3_ps, z_set, z_tok_ps, z_hat_set, out_ready = (
            sem("w3_ps"), sem("z_set"), sem("z_tok_ps"), sem("z_hat_set"), sem("out_ready"))

        x_chunks = x.rearrange("(c t p) d -> c p t d", p=P, t=TILES)
        out_chunks = out.rearrange("(c t p) d -> c p t d", p=P, t=TILES)

        def col(c, n=1):
            return vec[:, c:c + n]

        def cols(t):
            return slice(t * P, (t + 1) * P)

        def flat(buffer):
            return buffer[:, :, :].rearrange("p t d -> p (t d)")

        def follows_another(i):
            return not (isinstance(i, int) and i == 0)

        def x_norm_of(i):
            return ("x", i - 1, x_in) if follows_another(i) else ("x0", 0, x_res)

        def turn1_bank(i):
            return B_TURN if isinstance(i, int) and i == CHUNKS - 1 else B_TURN1

        block = ctx.enter_context(nc.Block())

        @block.sync
        def _(sp):
            def load_x(i):
                if follows_another(i) and not (isinstance(i, int) and i == 1):
                    sp.wait_ge(x_hat_set, i)
                    sp.wait_ge(x_normed, i)
                sp.dma_start(x_in[:, :, :], x_chunks[i]).then_inc(x_loaded, 16)

            def load_residual(i):
                if follows_another(i):
                    sp.wait_ge(x1_set, i)
                sp.dma_start(x_res[:, :, :], x_chunks[i]).then_inc(res_loaded, 16)

            def store(f):
                sp.wait_ge(out_ready, f + 1)
                sp.dma_start(out_chunks[f], y_out[:, :, :]).then_inc(out_free, 16)

            sp.sem_inc(out_free, 16)
            load_residual(0)
            sp.dma_start(vec[:, :], vectors).then_inc(vec_in, 16)
            sp.dma_start(att[:, 0:WOUT], att_w[:, 0:WOUT]).then_inc(att_in, 16)
            sp.dma_start(ident[:, :], identity).then_inc(ident_in, 16)
            load_x(1)
            sp.dma_start(att[:, WOUT:ATT_COLS], att_w[:, WOUT:ATT_COLS]).then_inc(out_w_in, 16)
            for p, (a, b) in enumerate(FFN_PIECES):
                sp.dma_start(ffn[:, a:b], ffn_w[:, a:b]).then_inc(ffn_in[p], 16)
            load_x(2)
            with sp.Fori(1, CHUNKS - 2) as i:
                load_residual(i)
                load_x(i + 2)
                store(i - 1)
            load_residual(CHUNKS - 2)
            store(CHUNKS - 3)
            load_residual(CHUNKS - 1)
            store(CHUNKS - 2)
            for f, (s, tiles, b) in HALVES:
                sp.wait_ge(out_ready, f + 1)
                sp.dma_start(out_chunks[CHUNKS - 1][:, tiles[0]:tiles[-1] + 1, :],
                             y_out[:, tiles[0]:tiles[-1] + 1, :]).then_inc(out_free, 16)
            sp.wait_ge(out_free, 16 * (CHUNKS + 2))

        @block.tensor
        def _(pe):
            def turn_x_hat(i):
                pe.wait_ge(x_hat_set, i + 1)
                for t in range(TILES):
                    last = pe.transpose(bank[B_TURN][:, cols(t)], x_hat[:, t, :], ident[:, :])
                last.then_inc(xt_ps, 1)

            def project_qk(i, after_projection=True):
                pe.wait_ge(xt_hi_set, i + 1)
                pe.wait_ge(xt_lo_set, i + 1)
                if after_projection and follows_another(i):
                    pe.wait_ge(y_att_set, i)
                ps = bank[B_TOK][:, :]
                w = slice(WQK, WQK + DIM)
                pe.matmul(ps, att_hi[:, w], xt_hi[:, :], start=True, stop=False)
                pe.matmul(ps, att_hi[:, w], xt_lo[:, :], start=False, stop=False)
                pe.matmul(ps, att_lo[:, w], xt_hi[:, :], start=False, stop=True).then_inc(qk_ps, 1)

            def project_v(i, tiles=range(TILES)):
                w = slice(WV, WV + HID)
                for t in tiles:
                    ps = bank[B_V[t // 2]][:, (t % 2) * HID:(t % 2 + 1) * HID]
                    pe.matmul(ps, xt_hi[:, cols(t)], att_hi[:, w], start=True, stop=False)
                    pe.matmul(ps, xt_lo[:, cols(t)], att_hi[:, w], start=False, stop=False)
                    pe.matmul(ps, xt_hi[:, cols(t)], att_lo[:, w], start=False, stop=False)
                    last = pe.matmul(ps, ones_r[:, :], bias_rows[:, :], start=False, stop=True)
                    if t % 2:
                        last.then_inc(v_ps, 1)

            def project_gate(i, blocks=range(KH)):
                for k in blocks:
                    ps = bank[B_GATE[k]][:, :]
                    w = slice(WG + k * P, WG + (k + 1) * P)
                    pe.matmul(ps, att_hi[:, w], xt_hi[:, :], start=True, stop=False)
                    pe.matmul(ps, att_hi[:, w], xt_lo[:, :], start=False, stop=False)
                    pe.matmul(ps, att_lo[:, w], xt_hi[:, :], start=False, stop=True).then_inc(gate_ps, 1)

            def turn_keys(i):
                pe.wait_ge(lin_k_head, i + 1)
                for t in range(TILES):
                    last = pe.transpose(bank[B_TURN][:, cols(t)], head_t[:, LIN_K, cols(t)], ident[:, :])
                last.then_inc(lin_k_ps, 1)

            def similarities(i):
                pe.wait_ge(quad_heads, i + 1)
                pe.wait_ge(gate_set, KH * i + 1)
                for t in range(TILES):
                    last = pe.matmul(bank[B_SIM][:, cols(t)], head_t[:, QUAD_K, cols(t)],
                                     head_t[:, QUAD_Q, cols(t)], start=True, stop=True)
                last.then_inc(sim_ps, 1)

            def keys_values(i):
                pe.wait_ge(lin_k_set, i + 1)
                pe.wait_ge(v_set, 2 * i + 2)
                pe.wait_ge(gate_set, KH * i + KH)
                for r in range(ROWS):
                    for t in range(2):
                        last = pe.matmul(bank[B_KV][:, r * HID:(r + 1) * HID], lin_k[:, 2 * r + t, :],
                                         v_tok[:, 2 * r + t, :], start=(t == 0), stop=(t == 1))
                last.then_inc(kv_ps, 1)

            def mix(i):
                pe.wait_ge(attn_set, i + 1)
                for k in range(KH):
                    for t in range(TILES):
                        pe.matmul(bank[B_GATE[k]][:, cols(t)], v_tok[:, t, k * P:(k + 1) * P],
                                  attn[:, t, :], start=(t == 0), stop=False)
                    if k == 0:
                        pe.wait_ge(kv_set, i + 1)
                        pe.wait_ge(lin_q_head, i + 1)
                    for r in range(ROWS):
                        last = pe.matmul(bank[B_GATE[k]][:, r * ROW:(r + 1) * ROW],
                                         lin_kv[:, r, k * P:(k + 1) * P],
                                         head_t[:, LIN_Q, r * ROW:(r + 1) * ROW],
                                         start=False, stop=(r == ROWS - 1))
                    last.then_inc(mix_ps, 1)

            def project_out(i):
                pe.wait_ge(gated_set, KH * i + KH)
                for t in range(TILES):
                    for k in range(KH):
                        last = pe.matmul(bank[B_TOK][:, cols(t)], gated_t[:, k, cols(t)],
                                         att[:, WOUT + k * DIM:WOUT + (k + 1) * DIM],
                                         start=(k == 0), stop=(k == KH - 1))
                last.then_inc(proj_ps, 1)

            def turn_x1_hat(i):
                pe.wait_ge(x1_hat_set, i + 1)
                if isinstance(i, int) and i == CHUNKS - 1:
                    pe.wait_ge(lin_k_set, CHUNKS)
                for t in range(TILES):
                    last = pe.transpose(bank[turn1_bank(i)][:, cols(t)], x1_hat[:, t, :], ident[:, :])
                last.then_inc(x1t_ps, 1)

            def weigh(ps, at, hi, lo, start, stop, with_lo):
                w = slice(at, at + P)
                pe.matmul(ps, ffn_hi[:, w], hi, start=start, stop=False)
                if with_lo:
                    pe.matmul(ps, ffn_lo[:, w], hi, start=False, stop=False)
                return pe.matmul(ps, ffn_hi[:, w], lo, start=False, stop=stop)

            def gated_layer(f, with_lo, part=WHOLE, blocks=range(KF)):
                s, tiles, b0 = part
                for m in blocks:
                    for at, b, done in ((W1, 2 * m % 4, w1_ps), (W2, 2 * m % 4 + 1, w2_ps)):
                        if m >= 2 and at == W1:
                            pe.wait_ge(silu_set, KF * f + m - 1)
                        if m >= 2 and at == W2:
                            pe.wait_ge(h0_set, KF * f + m - 1)
                        weigh(bank[b0 + b][:, s], at + m * P, x1t_hi[:, s], x1t_lo[:, s], True, True,
                              with_lo).then_inc(done, 1)

            def hidden_layer(f, at, hi, lo, hi_set, lo_set, done, blocks, with_lo, part):
                s, tiles, b0 = part

                def product(m, k):
                    return weigh(bank[b0 + m][:, s], at + k * FFN + m * P, hi[:, k, s], lo[:, k, s],
                                 k == 0, k == KF - 1, with_lo)

                early = [m for m in blocks if m < (2 if part is WHOLE else 1)]
                if early:
                    for k in range(KF - 1):
                        pe.wait_ge(hi_set, KF * f + k + 1)
                        pe.wait_ge(lo_set, KF * f + k + 1)
                        product(early[0], k)
                    for m in early[1:]:
                        for k in range(KF - 1):
                            product(m, k)
                    pe.wait_ge(hi_set, KF * f + KF)
                    pe.wait_ge(lo_set, KF * f + KF)
                    for m in early:
                        product(m, KF - 1).then_inc(done, 1)
                for m in blocks:
                    if m not in early:
                        for k in range(KF):
                            last = product(m, k)
                        last.then_inc(done, 1)

            def first_hidden_layer(f, with_lo, part=WHOLE, blocks=range(KF)):
                if 0 in blocks:
                    pe.wait_ge(silu_set, KF * f + KF)
                    pe.wait_ge(h0_set, KF * f + KF - 1)
                hidden_layer(f, H1, h0_hi, h0_lo, h0_hi_set, h0_lo_set, h1_ps, blocks, with_lo, part)

            def second_hidden_layer(f, with_lo, part=WHOLE):
                hidden_layer(f, H2, g1_hi, g1_lo, g1_hi_set, g1_lo_set, h2_ps, range(KF), with_lo, part)

            def last_layer(f, blocks, with_lo, part=WHOLE):
                s, tiles, b0 = part
                for k in blocks:
                    pe.wait_ge(g2_hi_set, KF * f + k + 1)
                    pe.wait_ge(g2_lo_set, KF * f + k + 1)
                    last = weigh(bank[b0 + B_LAST][:, s], W3 + k * DIM, g2_hi[:, k, s], g2_lo[:, k, s],
                                 k == 0, k == KF - 1, with_lo)
                if KF - 1 in blocks:
                    last.then_inc(w3_ps, 1)

            def turn_z(f, tiles, to_bank):
                pe.wait_ge(z_set, f + 1)
                for t in tiles:
                    last = pe.transpose(bank[to_bank][:, cols(t)], z_t[:, cols(t)], ident[:, :])
                last.then_inc(z_tok_ps, 1)

            def keep_busy(products):
                for n in range(products):
                    pe.matmul(bank[B_UNUSED][:, :], h0_hi[:, 0, 0:P], h0_hi[:, 0, :], start=True, stop=True)

            pe.wait_ge(consts_set, 1)
            keep_busy(WARM_UP)
            pe.wait_ge(rel_in, 48)
            pe.wait_ge(rel_wide_set, 1)
            for n in range(2):
                last = pe.matmul(bank[B_REL[n]][:, :], rel_wide[:, :], hot[:, n * CHUNK:(n + 1) * CHUNK],
                                 start=True, stop=True)
            last.then_inc(rel_ps, 1)
            pe.wait_ge(att_in, 16)
            pe.wait_ge(lnb_set, 1)
            pe.matmul(bank[B_BIAS][0:BR, 0:HID], lnb_pair[:, :], att[:, WV:WV + HID],
                      start=True, stop=True).then_inc(bias_ps, 1)
            for k in range(KH + 1):
                last = pe.matmul(bank[B_BIAS][:, HID + k:HID + k + 1], att[:, WG + k * P:WG + (k + 1) * P],
                                 col(C_LNB), start=True, stop=True)
            last.then_inc(bias_ps, 1)

            pe.wait_ge(ident_in, 16)
            turn_x_hat(0)
            keep_busy(3)
            pe.wait_ge(att_split, 1)
            project_qk(0)
            project_gate(0)
            pe.wait_ge(bias_split, 1)
            pe.wait_ge(gqk_set, 1)
            project_v(0)
            turn_x_hat(1)
            similarities(0)
            pe.wait_ge(xt_lo_set, 2)
            turn_keys(0)
            pe.wait_ge(qk_set, 1)
            project_qk(1, after_projection=False)
            keys_values(0)
            mix(0)
            project_v(1, range(TILES // 2))
            pe.wait_ge(out_w_in, 16)
            pe.wait_ge(qk_set, 2)
            project_out(0)
            project_v(1, range(TILES // 2, TILES))
            turn_keys(1)
            project_gate(1)
            similarities(1)
            keys_values(1)
            mix(1)
            pe.wait_ge(lo_summed, len(FFN_PIECES))
            pe.matmul(bank[0][0:1, 0:len(FFN_PIECES)], ones[:, :], lo_sums[:, :],
                      start=True, stop=True).then_inc(lo_ps, 1)
            turn_x1_hat(0)

            def steps(with_lo):
                def ffn_and_attention(i, ahead):
                    f = i - 1
                    pe.wait_ge(x1t_hi_set, f + 1)
                    pe.wait_ge(x1t_lo_set, f + 1)
                    gated_layer(f, with_lo)
                    project_out(i)
                    first_hidden_layer(f, with_lo, WHOLE, range(2))
                    if ahead:
                        turn_x_hat(i + 1)
                    first_hidden_layer(f, with_lo, WHOLE, range(2, KF))
                    if ahead:
                        pe.wait_ge(xt_hi_set, i + 2)
                        pe.wait_ge(xt_lo_set, i + 2)
                        project_gate(i + 1, [0])
                    second_hidden_layer(f, with_lo)
                    if ahead:
                        project_qk(i + 1)
                    else:
                        turn_x1_hat(i)
                    last_layer(f, range(KF - 1), with_lo)
                    if ahead:
                        project_v(i + 1, range(TILES // 2))
                    last_layer(f, [KF - 1], with_lo)
                    if ahead:
                        project_v(i + 1, range(TILES // 2, TILES))
                        pe.wait_ge(qk_set, i + 2)
                        turn_z(f, range(TILES), B_TOK)
                        turn_keys(i + 1)
                        project_gate(i + 1, [1])
                        similarities(i + 1)
                        keys_values(i + 1)
                        turn_x1_hat(i)
                        mix(i + 1)

                with pe.Fori(1, CHUNKS - 1) as i:
                    ffn_and_attention(i, True)
                ffn_and_attention(CHUNKS - 1, False)
                (fa, a), (fb, b) = HALVES
                pe.wait_ge(x1t_hi_set, CHUNKS)
                pe.wait_ge(x1t_lo_set, CHUNKS)
                pe.wait_ge(y_att_set, CHUNKS)
                gated_layer(fa, with_lo, a, range(KF // 2))
                turn_z(CHUNKS - 2, range(TILES), B_LAST_Z)
                gated_layer(fa, with_lo, a, range(KF // 2, KF))
                gated_layer(fb, with_lo, b, range(1))
                first_hidden_layer(fa, with_lo, a, range(KF // 2))
                pe.wait_ge(z_hat_set, CHUNKS - 1)
                gated_layer(fb, with_lo, b, range(1, KF))
                first_hidden_layer(fa, with_lo, a, range(KF // 2, KF))
                first_hidden_layer(fb, with_lo, b)
                second_hidden_layer(fa, with_lo, a)
                second_hidden_layer(fb, with_lo, b)
                last_layer(fa, range(KF), with_lo, a)
                last_layer(fb, range(KF), with_lo, b)
                for f, (s, tiles, b0) in HALVES:
                    turn_z(f, tiles, b0 + B_Z)

            pe.wait_ge(lo_flag_set, 1)
            has_lo = pe.value_load(lo_flag[0:1, 0:1], min_val=0, max_val=1)
            with pe.If(has_lo):
                steps(True)
            with pe.Else():
                steps(False)

        @block.scalar
        def _(act):
            def activations_qk(i):
                act.wait_ge(qk_ps, i + 1)
                act.activation(qk_t[:, :], bank[B_TOK][:, :], ACT.Silu,
                               bias=bias_gqk[:, KH:KH + 1]).then_inc(qk_set, 1)

            def activations_v(i):
                for n in range(2):
                    act.wait_ge(v_ps, 2 * i + n + 1)
                    act.activation(v_tok[:, 2 * n:2 * n + 2, :].rearrange("p t d -> p (t d)"),
                                   bank[B_V[n]][:, :], ACT.Silu).then_inc(v_set, 1)

            def copy_keys(i):
                act.wait_ge(lin_k_ps, i + 1)
                act.copy(flat(lin_k), bank[B_TURN][:, :]).then_inc(lin_k_set, 1)

            def activations_gate(i, blocks=range(KH)):
                for k in blocks:
                    act.wait_ge(gate_ps, KH * i + k + 1)
                    act.activation(gate_t[:, k, :], bank[B_GATE[k]][:, :], ACT.Silu,
                                   bias=bias_gqk[:, k:k + 1]).then_inc(gate_set, 1)

            def round_x_hat(i):
                act.wait_ge(xt_ps, i + 1)
                act.copy(xt_hi[:, :], bank[B_TURN][:, :]).then_inc(xt_hi_set, 1)

            def scale_kv(i):
                act.wait_ge(kv_ps, i + 1)
                act.mul(flat(lin_kv), bank[B_KV][:, :], 1.0 / ROW).then_inc(kv_set, 1)

            def round_ffn(p):
                a, b = FFN_PIECES[p]
                act.wait_ge(ffn_in[p], 16)
                act.copy(ffn_hi[:, a:b], ffn[:, a:b]).then_inc(ffn_rounded, 1)

            def sum_ffn_low(p):
                a, b = FFN_PIECES[p]
                act.wait_ge(ffn_split[p], 1)
                act.activation(ffn[:, a:b], ffn_lo[:, a:b].bitcast(F32), ACT.Abs,
                               accum_out=lo_sums[:, p:p + 1]).then_inc(lo_summed, 1)

            def round_x1_hat(i):
                act.wait_ge(x1t_ps, i + 1)
                act.copy(x1t_hi[:, :], bank[turn1_bank(i)][:, :]).then_inc(x1t_hi_set, 1)

            def silu_w1(f, part=WHOLE):
                s, tiles, b0 = part
                for m in range(KF):
                    act.wait_ge(w1_ps, KF * f + m + 1)
                    act.activation(silu_t[:, m, s], bank[b0 + 2 * m % 4][:, s], ACT.Silu,
                                   scale=col(C_S1 + m)).then_inc(silu_set, 1)

            def gelus(f, ps_done, scale, hi, hi_set, part=WHOLE, blocks=range(KF)):
                s, tiles, b0 = part
                for m in blocks:
                    act.wait_ge(ps_done, KF * f + m + 1)
                    act.activation(gelu_t[:, m, s], bank[b0 + m][:, s], ACT.Gelu,
                                   scale=col(scale + m))
                    act.activation(hi[:, m, s], bank[b0 + m][:, s], ACT.Gelu,
                                   scale=col(scale + m)).then_inc(hi_set, 1)

            def scale_z(f, part=WHOLE):
                s, tiles, b0 = part
                act.wait_ge(w3_ps, f + 1)
                act.mul(z_t[:, s], bank[b0 + B_LAST][:, s], col(C_S3)).then_inc(z_set, 1)

            act.dma_start(rel[:, :], rel_emb).then_inc(rel_in, 16)
            act.dma_start(hot[:, :], one_hot).then_inc(rel_in, 16)
            act.dma_start(own_key[:, :], own_keys).then_inc(rel_in, 16)
            act.wait_ge(consts_set, 1)
            for row in (0, GROUP):
                act.dma_start(bias_raw[row:row + 1, :], bias_v).then_inc(bias_in, 16)
            act.dma_start(bout[:, :], b_out.partition_broadcast(P)).then_inc(bout_in, 16)
            act.activation(unused[:, 0:1], ones[:, :], ACT.Silu)

            act.wait_ge(att_scaled, 1)
            act.copy(att_hi[:, :], att_g).then_inc(att_rounded, 1)
            round_x_hat(0)
            round_ffn(0)
            act.wait_ge(gqk_set, 1)
            activations_qk(0)
            activations_gate(0)
            activations_v(0)
            round_x_hat(1)
            round_ffn(1)
            copy_keys(0)
            act.wait_ge(lin_q_head, 1)
            act.wait_ge(quad_heads, 1)
            activations_qk(1)
            round_ffn(2)
            scale_kv(0)
            for p in range(3, len(FFN_PIECES)):
                round_ffn(p)
            sum_ffn_low(0)
            sum_ffn_low(1)
            activations_v(1)
            copy_keys(1)
            activations_gate(1)
            sum_ffn_low(2)
            scale_kv(1)
            for p in range(3, len(FFN_PIECES)):
                sum_ffn_low(p)
            round_x1_hat(0)

            def step(i, ahead):
                silu_w1(i - 1)
                gelus(i - 1, h1_ps, C_SH1, g1_hi, g1_hi_set, blocks=range(2))
                if ahead:
                    round_x_hat(i + 1)
                gelus(i - 1, h1_ps, C_SH1, g1_hi, g1_hi_set, blocks=range(2, KF))
                gelus(i - 1, h2_ps, C_SH2, g2_hi, g2_hi_set, blocks=range(KF - 1))
                if not ahead:
                    round_x1_hat(i)
                gelus(i - 1, h2_ps, C_SH2, g2_hi, g2_hi_set, blocks=[KF - 1])
                if ahead:
                    activations_qk(i + 1)
                    scale_z(i - 1)
                    activations_v(i + 1)
                    activations_gate(i + 1, [0])
                    copy_keys(i + 1)
                    activations_gate(i + 1, [1])
                    scale_kv(i + 1)
                    round_x1_hat(i)

            with act.Fori(1, CHUNKS - 1) as i:
                step(i, True)
            step(CHUNKS - 1, False)
            act.activation(unused[:, 1:2], ones[:, :], ACT.Silu)
            scale_z(CHUNKS - 2)
            for f, part in HALVES:
                silu_w1(f, part)
            for f, part in HALVES:
                gelus(f, h1_ps, C_SH1, g1_hi, g1_hi_set, part)
            for f, part in HALVES:
                gelus(f, h2_ps, C_SH2, g2_hi, g2_hi_set, part)
            for f, part in HALVES:
                scale_z(f, part)

        @block.vector
        def _(dve):
            def statistics(name, i, tile_of, tiles=range(TILES)):
                for t in tiles:
                    last = dve.bn_stats(bn[name][:, t, :], tile_of(t))
                last.then_inc(bn_done[name], 1)
                dve.wait_ge(bn_done[name], i + 1)
                dve.sem_inc(waits_passed, 1)
                for t in tiles:
                    last = dve.bn_aggr(mv[name][:, t, :], bn[name][:, t, :])
                last.then_inc(mv_done[name], 1)

            def normalize(name, to, tile_of, done, root=0, tiles=range(TILES)):
                for t in tiles:
                    last = dve.tensor_scalar(to[:, t, :], tile_of(t), mv[name][:, t, 0:1],
                                             rstd[name][:, root + t:root + t + 1],
                                             ALU.subtract, ALU.mult)
                last.then_inc(done, 1)

            def of(buffer):
                return lambda t: buffer[:, t, :]

            def of_bank(b):
                return lambda t: bank[b][:, cols(t)]

            def x_statistics(i):
                name, n, source = x_norm_of(i)
                if follows_another(i):
                    dve.wait_ge(x_loaded, 16 * i)
                else:
                    dve.wait_ge(res_loaded, 16)
                statistics(name, n, of(source))

            def x_normalize_twice(i):
                name, n, source = x_norm_of(i)
                dve.wait_ge(rstd_done[name], n + 1)
                normalize(name, x_hat, of(source), x_hat_set, root=TILES)

            def x_normalize(i):
                name, n, source = x_norm_of(i)
                if follows_another(i):
                    dve.wait_ge(norm_b_set, i)
                normalize(name, x_norm, of(source), x_normed)

            def low_x_hat(i):
                dve.wait_ge(xt_hi_set, i + 1)
                dve.tensor_tensor(xt_lo[:, :], bank[B_TURN][:, :], xt_hi[:, :].bitcast(F32),
                                  ALU.subtract).then_inc(xt_lo_set, 1)

            def heads(i):
                dve.wait_ge(qk_set, i + 1)
                for h, done in ((LIN_K, lin_k_head), (QUAD_K, None), (QUAD_Q, quad_heads)):
                    last = dve.tensor_scalar(head_t[:, h, :], qk_t[:, :], col(C_GAMMA + h),
                                             col(C_BETA + h), ALU.mult, ALU.add)
                    if done is not None:
                        last.then_inc(done, 1)

            def attention(i):
                dve.wait_ge(sim_ps, i + 1)
                dve.scalar_tensor_tensor(sim_b[:, :, :], bank[B_SIM][:, :].rearrange("p (t q) -> p t q", q=P),
                                         1.0 / GROUP, rel_bias[:, :].unsqueeze(1).broadcast_to([P, TILES, P]),
                                         ALU.mult, ALU.add).then_inc(sim_biased, 1)
                dve.wait_ge(sim_biased, i + 1)
                dve.scalar_tensor_tensor(flat(attn), flat(sim_b), 0.0, flat(sim_b),
                                         ALU.max, ALU.mult).then_inc(attn_set, 1)

            def gate_mix(i):
                for k in range(KH):
                    dve.wait_ge(mix_ps, KH * i + k + 1)
                    dve.tensor_tensor(gated_t[:, k, :], bank[B_GATE[k]][:, :], gate_t[:, k, :],
                                      ALU.mult).then_inc(gated_set, 1)

            def add_x_norm(i):
                dve.wait_ge(proj_ps, i + 1)
                dve.wait_ge(norm_b_set, i + 1)
                dve.tensor_tensor(flat(y_att), bank[B_TOK][:, :], flat(x_norm_b),
                                  ALU.add).then_inc(y_att_set, 1)
                dve.wait_ge(y_att_set, i + 1)
                statistics("att", i, of(y_att))

            def y_normalize(i):
                dve.wait_ge(rstd_done["att"], i + 1)
                normalize("att", y_hat, of(y_att), y_hat_set)

            def add_x(i):
                dve.wait_ge(y_hat_set, i + 1)
                dve.wait_ge(res_loaded, 16 * i + 16)
                if follows_another(i):
                    dve.wait_ge(x1_kept, i)
                dve.tensor_tensor(flat(x1), flat(y_hat), flat(x_res), ALU.add).then_inc(x1_set, 1)

            def x1_statistics(i):
                dve.wait_ge(x1_set, i + 1)
                statistics("x1", i, of(x1))

            def x1_normalize(i):
                dve.wait_ge(rstd_done["x1"], i + 1)
                normalize("x1", x1_hat, of(x1), x1_hat_set)

            def low_x1_hat(i):
                dve.wait_ge(x1t_hi_set, i + 1)
                dve.tensor_tensor(x1t_lo[:, :], bank[turn1_bank(i)][:, :], x1t_hi[:, :].bitcast(F32),
                                  ALU.subtract).then_inc(x1t_lo_set, 1)

            def gated_product(f, m, part=WHOLE):
                s, tiles, b0 = part
                dve.wait_ge(silu_set, KF * f + m + 1)
                dve.wait_ge(w2_ps, KF * f + m + 1)
                dve.scalar_tensor_tensor(h0[:, m, s], bank[b0 + 2 * m % 4 + 1][:, s], col(C_S2 + m),
                                         silu_t[:, m, s], ALU.mult, ALU.mult).then_inc(h0_set, 1)

            def low_h0(f, m, part=WHOLE):
                s, tiles, b0 = part
                dve.wait_ge(h0_hi_set, KF * f + m + 1)
                dve.tensor_tensor(h0_lo[:, m, s], h0[:, m, s], h0_hi[:, m, s].bitcast(F32),
                                  ALU.subtract).then_inc(h0_lo_set, 1)

            def gated_layer(f, part=WHOLE):
                gated_product(f, 0, part)
                for m in range(1, KF):
                    gated_product(f, m, part)
                    low_h0(f, m - 1, part)
                low_h0(f, KF - 1, part)

            def low_gelu(f, m, hi, lo, hi_set, lo_set, part=WHOLE):
                s, tiles, b0 = part
                dve.wait_ge(hi_set, KF * f + m + 1)
                dve.tensor_tensor(lo[:, m, s], gelu_t[:, m, s], hi[:, m, s].bitcast(F32),
                                  ALU.subtract).then_inc(lo_set, 1)

            def z_statistics(f, b=B_TOK, tiles=range(TILES)):
                dve.wait_ge(z_tok_ps, f + 1)
                statistics("ffn", f, of_bank(b), tiles)

            def z_normalize(f, b=B_TOK, tiles=range(TILES)):
                dve.wait_ge(rstd_done["ffn"], f + 1)
                normalize("ffn", z_hat, of_bank(b), z_hat_set, tiles=tiles)

            dve.memset(h0_hi[:, 0, :].bitcast(F32), 1.0)
            dve.memset(minus_half[:, :], -0.5)
            dve.memset(ones[:, :], 1.0)
            dve.memset(ones_r[:, :].bitcast(F32), 1.0)
            dve.memset(lnb_pair[:, :], 0.0)
            dve.memset(rel_bias[:, :], MASKED)
            dve.memset(bias_raw[:, :], 0.0).then_inc(consts_set, 1)
            x_statistics(0)
            dve.wait_ge(consts_set, 1)
            dve.wait_ge(vec_in, 16)
            for c in (0, GROUP):
                last = dve.tensor_copy(lnb_pair[:, c:c + 1], col(C_LNB))
            last.then_inc(lnb_set, 1)
            dve.wait_ge(rel_in, 48)
            dve.tensor_scalar(rel_wide[:, :], rel[:, 0:1].broadcast_to([BUCKETS, P]), 1.0, None,
                              ALU.mult).then_inc(rel_wide_set, 1)
            dve.wait_ge(att_in, 16)
            dve.tensor_scalar(att_g, att[:, 0:WOUT], col(C_LNG), None, ALU.mult).then_inc(att_scaled, 1)
            x_normalize_twice(0)
            dve.wait_ge(att_rounded, 1)
            dve.tensor_tensor(att_lo[:, :], att_g, att_hi[:, :].bitcast(F32),
                              ALU.subtract).then_inc(att_split, 1)
            dve.wait_ge(bias_ps, 2)
            dve.wait_ge(bias_in, 32)
            dve.tensor_tensor(bias_gqk[:, :], bank[B_BIAS][:, HID:HID + KH + 1], col(C_BG, KH + 1), ALU.add).then_inc(gqk_set, 1)
            dve.tensor_tensor(bias_sum[:, :], bank[B_BIAS][0:BR, 0:HID], bias_raw[:, :], ALU.add).then_inc(bias_added, 1)
            low_x_hat(0)
            x_statistics(1)
            dve.wait_ge(bias_added, 1)
            dve.tensor_copy(bias_rnd[:, :], bias_sum[:, :])
            dve.tensor_copy(bias_rows[:, :], bias_sum[:, :]).then_inc(bias_added, 1)
            dve.wait_ge(bias_added, 2)
            dve.tensor_tensor(bias_rows[GROUP:BR, :], bias_sum[GROUP:BR, :],
                              bias_rnd[GROUP:BR, :].bitcast(F32), ALU.subtract).then_inc(bias_split, 1)
            x_normalize_twice(1)
            heads(0)
            dve.wait_ge(rel_ps, 1)
            half = GROUP // 2
            for n in range(2):
                last = dve.tensor_tensor(rel_picked[:, n * half:(n + 1) * half, :],
                                         bank[B_REL[n]][:, :].rearrange("p (q k) -> p q k", k=GROUP),
                                         own_key[:, :].unsqueeze(1).broadcast_to([P, half, GROUP]), ALU.mult)
            last.then_inc(rel_set, 1)
            low_x_hat(1)
            dve.wait_ge(rel_set, 1)
            dve.reduce_sum(rel_group[:, :], rel_picked, AX_X).then_inc(rel_set, 1)
            dve.wait_ge(rel_set, 2)
            for g in range(P // GROUP):
                s = slice(g * GROUP, (g + 1) * GROUP)
                last = dve.tensor_scalar(rel_bias[s, s], rel_group[s, :], float(DIM) ** 0.5, None, ALU.mult)
            last.then_inc(rel_set, 1)
            dve.wait_ge(rel_set, 3)
            attention(0)
            heads(1)
            x_normalize(0)
            gate_mix(0)
            for p in range(PIECES_OF_POOL, len(FFN_PIECES)):
                a, b = FFN_PIECES[p]
                dve.wait_ge(ffn_rounded, p + 1)
                dve.tensor_tensor(ffn_lo[:, a:b], ffn[:, a:b], ffn_hi[:, a:b].bitcast(F32),
                                  ALU.subtract).then_inc(ffn_split[p], 1)
            add_x_norm(0)
            x_normalize(1)
            y_normalize(0)
            add_x(0)
            attention(1)
            x1_statistics(0)
            x1_normalize(0)
            dve.wait_ge(lo_ps, 1)
            dve.reduce_sum(lo_total[:, :], bank[0][0:1, 0:len(FFN_PIECES)], AX_X).then_inc(lo_total_set, 1)
            dve.wait_ge(lo_total_set, 1)
            dve.tensor_scalar(lo_flag[:, :], lo_total[:, :], 0.0, None, ALU.is_gt).then_inc(lo_flag_set, 1)
            low_x1_hat(0)

            def low_gelu1(f, m):
                low_gelu(f, m, g1_hi, g1_lo, g1_hi_set, g1_lo_set)

            def low_gelu2(f, m):
                low_gelu(f, m, g2_hi, g2_lo, g2_hi_set, g2_lo_set)

            def step(i, ahead):
                f = i - 1
                if ahead:
                    x_statistics(i + 1)
                gate_mix(i)
                gated_layer(f)
                if ahead:
                    x_normalize_twice(i + 1)
                add_x_norm(i)
                low_gelu1(f, 0)
                low_gelu1(f, 1)
                y_normalize(i)
                if ahead:
                    low_x_hat(i + 1)
                low_gelu1(f, 2)
                add_x(i)
                low_gelu1(f, 3)
                x1_statistics(i)
                if ahead:
                    x_normalize(i + 1)
                    low_gelu2(f, 0)
                    low_gelu2(f, 1)
                    x1_normalize(i)
                else:
                    x1_normalize(i)
                    low_gelu2(f, 0)
                    low_gelu2(f, 1)
                low_gelu2(f, 2)
                if not ahead:
                    low_x1_hat(i)
                low_gelu2(f, 3)
                if ahead:
                    heads(i + 1)
                    z_statistics(f)
                    attention(i + 1)
                    z_normalize(f)
                    low_x1_hat(i)

            with dve.Fori(1, CHUNKS - 1) as i:
                step(i, True)
            step(CHUNKS - 1, False)
            (fa, a), (fb, b) = HALVES
            gated_product(fa, 0, a)
            gated_product(fa, 1, a)
            low_h0(fa, 0, a)
            gated_product(fa, 2, a)
            low_h0(fa, 1, a)
            z_statistics(CHUNKS - 2, B_LAST_Z)
            gated_product(fa, 3, a)
            low_h0(fa, 2, a)
            low_h0(fa, 3, a)
            z_normalize(CHUNKS - 2, B_LAST_Z)
            gated_layer(fb, b)
            for hi, lo, hi_set, lo_set in ((g1_hi, g1_lo, g1_hi_set, g1_lo_set),
                                           (g2_hi, g2_lo, g2_hi_set, g2_lo_set)):
                for f, part in HALVES:
                    for m in range(KF):
                        low_gelu(f, m, hi, lo, hi_set, lo_set, part)
            for f, (s, tiles, b0) in HALVES:
                z_statistics(f, b0 + B_Z, tiles)
            for f, (s, tiles, b0) in HALVES:
                z_normalize(f, b0 + B_Z, tiles)

        @block.gpsimd
        def _(pool):
            def after(semaphore, value):
                pool.wait_ge(semaphore, value)
                pool.sem_inc(waits_passed, 1)

            def root(name, i, twice=False, tiles=range(TILES)):
                after(mv_done[name], i + 1)
                a, b = tiles[0], tiles[-1] + 1
                last = pool.tensor_scalar(arg[name][:, a:b], mv[name][:, a:b, 1], 1.0, EPS,
                                          ALU.mult, ALU.add)
                if twice:
                    last = pool.tensor_scalar(arg[name][:, TILES:2 * TILES], mv[name][:, :, 1], 1.0 + EPS,
                                              EPS * EPS, ALU.mult, ALU.add)
                    b = 2 * TILES
                last.then_inc(arg_done[name], 1)
                pool.wait_ge(arg_done[name], i + 1)
                pool.tensor_tensor(rstd[name][:, a:b], arg[name][:, a:b], minus_half[:, a:b],
                                   ALU.pow).then_inc(rstd_done[name], 1)

            def root_x(i):
                name, n, source = x_norm_of(i)
                root(name, n, twice=True)

            def add_b_out(i):
                pool.wait_ge(x_normed, i + 1)
                if follows_another(i):
                    pool.wait_ge(y_att_set, i)
                pool.tensor_tensor(x_norm_b[:, :, :], x_norm[:, :, :],
                                   bout[:, :].unsqueeze(1).broadcast_to([P, TILES, DIM]),
                                   ALU.add).then_inc(norm_b_set, 1)

            def lin_q(i):
                after(qk_set, i + 1)
                pool.tensor_scalar(head_t[:, LIN_Q, :], qk_t[:, :], col(C_GAMMA + LIN_Q),
                                   col(C_BETA + LIN_Q), ALU.mult, ALU.add).then_inc(lin_q_head, 1)

            def round_h0(f, part=WHOLE, blocks=range(KF)):
                s, tiles, b0 = part
                for m in blocks:
                    after(h0_set, KF * f + m + 1)
                    pool.tensor_scalar(h0_hi[:, m, s], h0[:, m, s], 1.0, 0.0,
                                       ALU.mult, ALU.add).then_inc(h0_hi_set, 1)

            def keep_x1(f):
                if follows_another(f):
                    pool.wait_ge(out_ready, f)
                after(x1_set, f + 1)
                pool.tensor_scalar(flat(x1_res), flat(x1), 1.0, 0.0, ALU.mult, ALU.add).then_inc(x1_kept, 1)

            def make_out(f):
                pool.wait_ge(z_hat_set, f + 1)
                pool.wait_ge(out_free, 16 * f + 16)
                pool.tensor_tensor(flat(y_out), flat(z_hat), flat(x1_res), ALU.add).then_inc(out_ready, 1)

            pool.wait_ge(consts_set, 1)
            root_x(0)
            pool.wait_ge(vec_in, 16)
            pool.wait_ge(bout_in, 16)
            root_x(1)
            lin_q(0)

            def low_ffn(p):
                a, b = FFN_PIECES[p]
                pool.wait_ge(ffn_rounded, p + 1)
                pool.tensor_tensor(ffn_lo[:, a:b], ffn[:, a:b], ffn_hi[:, a:b].bitcast(F32),
                                   ALU.subtract).then_inc(ffn_split[p], 1)

            low_ffn(0)
            low_ffn(1)
            low_ffn(2)
            add_b_out(0)
            pool.wait_ge(mix_ps, KH)
            lin_q(1)
            low_ffn(3)
            root("att", 0)
            root("x1", 0)
            keep_x1(0)
            add_b_out(1)

            def step(i, ahead):
                if ahead:
                    root_x(i + 1)
                round_h0(i - 1)
                root("att", i)
                root("x1", i)
                if ahead:
                    add_b_out(i + 1)
                    lin_q(i + 1)
                    root("ffn", i - 1)
                    make_out(i - 1)
                    keep_x1(i)

            with pool.Fori(1, CHUNKS - 1) as i:
                step(i, True)
            step(CHUNKS - 1, False)
            (fa, a), (fb, b) = HALVES
            round_h0(fa, a, range(KF - 1))
            root("ffn", CHUNKS - 2)
            round_h0(fa, a, [KF - 1])
            round_h0(fb, b)
            make_out(CHUNKS - 2)
            keep_x1(CHUNKS - 1)
            for f, (s, tiles, b0) in HALVES:
                root("ffn", f, tiles=tiles)
            for f, (s, tiles, b0) in HALVES:
                pool.wait_ge(z_hat_set, f + 1)
                pool.wait_ge(out_free, 16 * CHUNKS)
                a, b = tiles[0], tiles[-1] + 1
                pool.tensor_tensor(y_out[:, a:b, :], z_hat[:, a:b, :], x1_res[:, a:b, :],
                                   ALU.add).then_inc(out_ready, 1)


def _bucket_table():
    pos = np.arange(GROUP)
    n = -(pos[None, :] - pos[:, None])
    nb = BUCKETS // 2
    ret = (n < 0).astype(np.int32) * nb
    n = np.abs(n)
    exact = nb // 2
    ratio = np.log(np.maximum(n, 1).astype(np.float32) / np.float32(exact)) / np.float32(np.log(MAX_DIST / exact))
    large = exact + (ratio * np.float32(nb - exact)).astype(np.int32)
    return ret + np.where(n < exact, n, np.minimum(large, nb - 1))


def _one_hot():
    hot = _bucket_table()[None, :, :] == np.arange(BUCKETS)[:, None, None]
    return hot.reshape(BUCKETS, -1).astype(np.float32)


def _blocks(w):
    o, n = w.shape
    return w.T.reshape(n // P, P, o).transpose(1, 0, 2).reshape(P, -1)


def _columns(v):
    return v.reshape(-1, P).T


def kernel(**inputs):
    import concourse.bacc as _bacc
    from concourse.bass_utils import run_bass_kernel_spmd as _run

    a = {k.removeprefix("L0_"): np.asarray(v) for k, v in inputs.items()}
    w_h, b_h = a["attn_W_h"], a["attn_b_h"]
    w_out = a["attn_W_out"].reshape(KH, P, DIM).transpose(1, 0, 2).reshape(P, -1)
    layout = {
        "x": a["attn_x"].reshape(TOKENS, DIM),
        "att_w": np.concatenate([w_h, a["attn_W_qk"], w_out], axis=1),
        "ffn_w": np.concatenate([_blocks(a[f"ffn_{n}_w"]) for n in ("w1", "w2", "h1", "h2", "w3")], axis=1),
        "vectors": np.concatenate(
            [_columns(v) for v in (a["attn_ln_g"], a["attn_ln_b"], b_h[HID:], a["attn_b_qk"],
                                   a["attn_os_gamma"], a["attn_os_beta"], a["ffn_w1_s"], a["ffn_w2_s"],
                                   a["ffn_h1_s"], a["ffn_h2_s"], a["ffn_w3_s"])], axis=1),
        "bias_v": b_h[:HID].reshape(1, HID),
        "b_out": a["attn_b_out"].reshape(1, DIM),
        "rel_emb": a["attn_rel_emb"],
        "one_hot": _one_hot(),
        "own_keys": np.tile(np.eye(GROUP, dtype=np.float32), (P // GROUP, 1)),
        "identity": np.eye(P, dtype=np.float32),
    }
    nc = _bacc.Bacc("TRN2", target_bir_lowering=False, num_devices=1)
    arrays, args = {}, []
    for name, v in layout.items():
        v = np.ascontiguousarray(v)
        arrays[f"in_{name}"] = v
        args.append(nc.dram_tensor(f"in_{name}", v.shape, F32, kind="ExternalInput").ap())
    out = nc.dram_tensor("out_x", (TOKENS, DIM), F32, kind="ExternalOutput").ap()
    build(nc, *args, out)
    r = _run(nc, [arrays], core_ids=[0])
    return r.results[0]["out_x"].reshape(inputs["L0_attn_x"].shape)
```

```python
from contextlib import ExitStack

import numpy as np

import concourse.bass as bass
from concourse import mybir

P = 128
DIM = 128
HID = 256
FFN = 512
TOKENS = 4096
ROW = 256
GROUP = 32
CHUNK = 512
CHUNKS = TOKENS // CHUNK
TILES = CHUNK // P
ROWS = CHUNK // ROW
KF = FFN // P
KH = HID // P
BUCKETS = 32
MAX_DIST = 128
EPS = 1e-5
KEEP_BUSY = 1
WARM_UP = 9
MASKED = -1e38

W1, W2, H1, H2, W3 = 0, FFN, 2 * FFN, 2 * FFN + KF * FFN, 2 * FFN + 2 * KF * FFN
FFN_COLS = W3 + KF * DIM
FFN_PIECES = [(c, min(c + 2 * FFN, FFN_COLS)) for c in range(0, FFN_COLS, 2 * FFN)]
PIECES_OF_POOL = 4
WV, WG, WQK, WOUT = 0, HID, 2 * HID, 2 * HID + DIM
ATT_COLS = WOUT + KH * DIM
C_LNG, C_LNB, C_BG, C_BQK, C_GAMMA, C_BETA = 0, 1, 2, 4, 5, 9
C_S1, C_S2, C_SH1, C_SH2, C_S3 = 13, 17, 21, 25, 29
VEC_COLS = 30
QUAD_Q, LIN_Q, QUAD_K, LIN_K = range(4)

WHOLE = (slice(0, CHUNK), range(TILES), 0)
HALVES = [(CHUNKS - 1 + h, (slice(h * ROW, (h + 1) * ROW), range(2 * h, 2 * h + 2), 4 - 4 * h))
          for h in range(2)]

F32 = mybir.dt.float32
F32R = mybir.dt.float32r
I32 = mybir.dt.int32
ALU = mybir.AluOpType
ACT = mybir.ActivationFunctionType
AX_X = mybir.AxisListType.X


def build(nc, x, att_w, ffn_w, vectors, bias_v, b_out, rel_emb, one_hot, own_keys, identity, out):
    ctx = ExitStack()
    with ctx:
        def sb(name, shape, dt=F32):
            return ctx.enter_context(nc.sbuf_tensor(name, shape, dt))

        def sem(name):
            return ctx.enter_context(nc.semaphore(name))

        att = sb("att", [P, ATT_COLS])
        att_hi = sb("att_hi", [P, WOUT], F32R)
        att_lo = sb("att_lo", [P, WOUT], F32R)
        ffn = sb("ffn", [P, FFN_COLS])
        ffn_hi = sb("ffn_hi", [P, FFN_COLS], F32R)
        ffn_lo = sb("ffn_lo", [P, FFN_COLS], F32R)
        vec = sb("vec", [P, VEC_COLS])
        ident = sb("ident", [P, P])
        hot = sb("hot", [BUCKETS, GROUP * GROUP])
        own_key = sb("own_key", [P, GROUP])
        rel = sb("rel", [BUCKETS, 1])
        rel_wide = sb("rel_wide", [BUCKETS, P])
        rel_group = sb("rel_group", [P, GROUP])
        rel_bias = sb("rel_bias", [P, P])
        bout = sb("bout", [P, DIM])
        BR = GROUP + 1
        lnb_pair = sb("lnb_pair", [P, BR])
        bias_raw = sb("bias_raw", [BR, HID])
        bias_sum = sb("bias_sum", [BR, HID])
        bias_rnd = sb("bias_rnd", [BR, HID], F32R)
        bias_rows = sb("bias_rows", [BR, HID], F32R)
        ones_r = sb("ones_r", [BR, P], F32R)
        bias_gqk = sb("bias_gqk", [P, KH + 1])
        ones = sb("ones", [P, 1])
        unused = sb("unused", [P, 1])
        minus_half = sb("minus_half", [P, 2 * TILES])
        lo_sums = sb("lo_sums", [P, len(FFN_PIECES)])
        lo_total = sb("lo_total", [1, 1])
        lo_flag = sb("lo_flag", [1, 1], I32)

        x_in = sb("x_in", [P, TILES, DIM])
        x_res = sb("x_res", [P, TILES, DIM])
        x_norm = sb("x_norm", [P, TILES, DIM])
        x_norm_b = sb("x_norm_b", [P, TILES, DIM])
        x_hat = sb("x_hat", [P, TILES, DIM])
        xt_hi = sb("xt_hi", [P, CHUNK], F32R)
        xt_lo = sb("xt_lo", [P, CHUNK], F32R)
        qk_t = sb("qk_t", [P, CHUNK])
        v_tok = sb("v_tok", [P, TILES, HID])
        gate_t = sb("gate_t", [P, KH, CHUNK])
        head_t = sb("head_t", [P, 4, CHUNK])
        sim_b = sb("sim_b", [P, TILES, P])
        attn = sb("attn", [P, TILES, P])
        weights = sb("weights", [P, ROWS, 4, P])
        same_tile, other_tile = weights[:, :, 0:4:3, :], weights[:, :, 1:3, :]
        gated_t = sb("gated_t", [P, KH, CHUNK])
        y_att = sb("y_att", [P, TILES, DIM])
        y_hat = sb("y_hat", [P, TILES, DIM])
        x1 = sb("x1", [P, TILES, DIM])
        x1_hat = sb("x1_hat", [P, TILES, DIM])
        x1_res = sb("x1_res", [P, TILES, DIM])
        x1t_hi = sb("x1t_hi", [P, CHUNK], F32R)
        x1t_lo = sb("x1t_lo", [P, CHUNK], F32R)
        silu_h0 = sb("silu_h0", [P, 2 * KF, CHUNK])
        silu_t, h0 = silu_h0[:, 0:KF, :], silu_h0[:, KF:2 * KF, :]
        rel_picked = silu_h0[:, 0:2, :].rearrange("p m n -> p (m n)").rearrange(
            "p (q k) -> p q k", k=GROUP)
        rel_all = silu_h0[:, 2:4, :].rearrange("p m n -> p (m n)").rearrange(
            "p (q k) -> p q k", k=GROUP)
        h0_hi = sb("h0_hi", [P, KF, CHUNK], F32R)
        h0_lo = sb("h0_lo", [P, KF, CHUNK], F32R)
        gelu_t = sb("gelu_t", [P, KF, CHUNK])
        att_g = gelu_t[:, 0:2, :].rearrange("p m n -> p (m n)")[:, 0:WOUT]
        g1_hi = sb("g1_hi", [P, KF, CHUNK], F32R)
        g1_lo = sb("g1_lo", [P, KF, CHUNK], F32R)
        g2_hi, g2_lo = h0_hi, h0_lo
        z_t = sb("z_t", [P, CHUNK])
        z_hat = sb("z_hat", [P, TILES, DIM])
        z_tok = x_norm
        y_out = sb("y_out", [P, TILES, DIM])
        NORMS = ("x0", "x", "att", "x1", "ffn")
        bn = {n: sb(f"bn_{n}", [P, TILES, 6]) for n in NORMS}
        mv = {n: sb(f"mv_{n}", [P, TILES, 2]) for n in NORMS}
        arg = {n: sb(f"arg_{n}", [P, 2 * TILES]) for n in NORMS}
        rstd = {n: sb(f"rstd_{n}", [P, 2 * TILES]) for n in NORMS}

        bank = [ctx.enter_context(nc.psum_tensor(f"bank{b}", [P, CHUNK], F32)) for b in range(8)]
        B_LAST, B_V, B_GATE, B_SIM, B_TURN, B_TURN1, B_TOK = 0, (1, 2), (4, 5), 5, 6, 0, 7
        B_SAME, B_OTHER = 6, 3
        B_REL, B_BIAS, B_SPARE = (3, 0), 2, 1
        B_SAME0 = 0
        B_LAST_Z, B_Z = 3, 1

        vec_in, att_in, x_loaded, res_loaded = sem("vec_in"), sem("att_in"), sem("x_loaded"), sem("res_loaded")
        rel_in, ident_in, bout_in, bias_in = sem("rel_in"), sem("ident_in"), sem("bout_in"), sem("bias_in")
        ffn_in = [sem(f"ffn_in{p}") for p in range(len(FFN_PIECES))]
        out_w_in = sem("out_w_in")
        out_free = sem("out_free")
        waits_passed = sem("waits_passed")
        consts_set, att_scaled, att_rounded, att_split = (
            sem("consts_set"), sem("att_scaled"), sem("att_rounded"), sem("att_split"))
        lnb_set, bias_ps, bias_added, bias_split = sem("lnb_set"), sem("bias_ps"), sem("bias_added"), sem("bias_split")
        rel_wide_set, rel_ps, rel_all_set, rel_set, gqk_set = (
            sem("rel_wide_set"), sem("rel_ps"), sem("rel_all_set"), sem("rel_set"), sem("gqk_set"))
        ffn_rounded, lo_summed, lo_ps, lo_total_set, lo_flag_set = (
            sem("ffn_rounded"), sem("lo_summed"), sem("lo_ps"), sem("lo_total_set"), sem("lo_flag_set"))
        ffn_split = [sem(f"ffn_split{p}") for p in range(len(FFN_PIECES))]
        bn_done = {n: sem(f"bn_done_{n}") for n in bn}
        mv_done = {n: sem(f"mv_done_{n}") for n in bn}
        arg_done = {n: sem(f"arg_done_{n}") for n in bn}
        rstd_done = {n: sem(f"rstd_done_{n}") for n in bn}
        x_normed, x_hat_set, norm_b_set = sem("x_normed"), sem("x_hat_set"), sem("norm_b_set")
        xt_ps, xt_hi_set, xt_lo_set = sem("xt_ps"), sem("xt_hi_set"), sem("xt_lo_set")
        qk_ps, v_ps, gate_ps = sem("qk_ps"), sem("v_ps"), sem("gate_ps")
        qk_set, v_set, gate_set = sem("qk_set"), sem("v_set"), sem("gate_set")
        quad_heads, lin_heads = sem("quad_heads"), sem("lin_heads")
        same_ps, same_set, other_ps, other_set = sem("same_ps"), sem("same_set"), sem("other_ps"), sem("other_set")
        sim_ps, sim_biased, attn_set = sem("sim_ps"), sem("sim_biased"), sem("attn_set")
        mix_ps, gated_set = sem("mix_ps"), sem("gated_set")
        proj_ps, y_att_set, y_hat_set, x1_set, x1_hat_set = (
            sem("proj_ps"), sem("y_att_set"), sem("y_hat_set"), sem("x1_set"), sem("x1_hat_set"))
        x1_kept, x1t_ps, x1t_hi_set, x1t_lo_set = (
            sem("x1_kept"), sem("x1t_ps"), sem("x1t_hi_set"), sem("x1t_lo_set"))
        w1_ps, w2_ps, silu_set = sem("w1_ps"), sem("w2_ps"), sem("silu_set")
        h0_set, h0_hi_set, h0_lo_set = sem("h0_set"), sem("h0_hi_set"), sem("h0_lo_set")
        h1_ps, g1_hi_set, g1_lo_set = sem("h1_ps"), sem("g1_hi_set"), sem("g1_lo_set")
        h2_ps, g2_hi_set, g2_lo_set = sem("h2_ps"), sem("g2_hi_set"), sem("g2_lo_set")
        w3_ps, z_set, z_tok_ps, z_copied, z_hat_set, out_ready = (
            sem("w3_ps"), sem("z_set"), sem("z_tok_ps"), sem("z_copied"), sem("z_hat_set"), sem("out_ready"))

        x_chunks = x.rearrange("(c t p) d -> c p t d", p=P, t=TILES)
        out_chunks = out.rearrange("(c t p) d -> c p t d", p=P, t=TILES)

        def col(c, n=1):
            return vec[:, c:c + n]

        def cols(t):
            return slice(t * P, (t + 1) * P)

        def flat(buffer):
            return buffer[:, :, :].rearrange("p t d -> p (t d)")

        def follows_another(i):
            return not (isinstance(i, int) and i == 0)

        def x_norm_of(i):
            return ("x", i - 1, x_in) if follows_another(i) else ("x0", 0, x_res)

        def same_bank(i):
            return B_SAME if follows_another(i) else B_SAME0

        def turn1_bank(i):
            return B_TURN if isinstance(i, int) and i == CHUNKS - 1 else B_TURN1

        block = ctx.enter_context(nc.Block())

        @block.sync
        def _(sp):
            def load_x(i):
                if follows_another(i) and not (isinstance(i, int) and i == 1):
                    sp.wait_ge(x_hat_set, i)
                    sp.wait_ge(x_normed, i)
                sp.dma_start(x_in[:, :, :], x_chunks[i]).then_inc(x_loaded, 16)

            def load_residual(i):
                if follows_another(i):
                    sp.wait_ge(x1_set, i)
                sp.dma_start(x_res[:, :, :], x_chunks[i]).then_inc(res_loaded, 16)

            def store(f):
                sp.wait_ge(out_ready, f + 1)
                sp.dma_start(out_chunks[f], y_out[:, :, :]).then_inc(out_free, 16)

            sp.sem_inc(out_free, 16)
            load_residual(0)
            sp.dma_start(vec[:, :], vectors).then_inc(vec_in, 16)
            sp.dma_start(att[:, 0:WOUT], att_w[:, 0:WOUT]).then_inc(att_in, 16)
            sp.dma_start(ident[:, :], identity).then_inc(ident_in, 16)
            load_x(1)
            sp.dma_start(att[:, WOUT:ATT_COLS], att_w[:, WOUT:ATT_COLS]).then_inc(out_w_in, 16)
            for p, (a, b) in enumerate(FFN_PIECES):
                sp.dma_start(ffn[:, a:b], ffn_w[:, a:b]).then_inc(ffn_in[p], 16)
            load_x(2)
            with sp.Fori(1, CHUNKS - 2) as i:
                load_residual(i)
                load_x(i + 2)
                store(i - 1)
            load_residual(CHUNKS - 2)
            store(CHUNKS - 3)
            load_residual(CHUNKS - 1)
            store(CHUNKS - 2)
            for f, (s, tiles, b) in HALVES:
                sp.wait_ge(out_ready, f + 1)
                sp.dma_start(out_chunks[CHUNKS - 1][:, tiles[0]:tiles[-1] + 1, :],
                             y_out[:, tiles[0]:tiles[-1] + 1, :]).then_inc(out_free, 16)
            sp.wait_ge(out_free, 16 * (CHUNKS + 2))

        @block.tensor
        def _(pe):
            def turn_x_hat(i):
                pe.wait_ge(x_hat_set, i + 1)
                for t in range(TILES):
                    last = pe.transpose(bank[B_TURN][:, cols(t)], x_hat[:, t, :], ident[:, :])
                last.then_inc(xt_ps, 1)

            def project_qk(i, bank_is_free=False):
                pe.wait_ge(xt_hi_set, i + 1)
                pe.wait_ge(xt_lo_set, i + 1)
                if follows_another(i) and not bank_is_free:
                    pe.wait_ge(y_att_set, i)
                ps = bank[B_TOK][:, :]
                w = slice(WQK, WQK + DIM)
                pe.matmul(ps, att_hi[:, w], xt_hi[:, :], start=True, stop=False)
                pe.matmul(ps, att_hi[:, w], xt_lo[:, :], start=False, stop=False)
                pe.matmul(ps, att_lo[:, w], xt_hi[:, :], start=False, stop=True).then_inc(qk_ps, 1)

            def project_v(i, tiles=range(TILES)):
                w = slice(WV, WV + HID)
                for t in tiles:
                    ps = bank[B_V[t // 2]][:, (t % 2) * HID:(t % 2 + 1) * HID]
                    pe.matmul(ps, xt_hi[:, cols(t)], att_hi[:, w], start=True, stop=False)
                    pe.matmul(ps, xt_lo[:, cols(t)], att_hi[:, w], start=False, stop=False)
                    pe.matmul(ps, xt_hi[:, cols(t)], att_lo[:, w], start=False, stop=False)
                    last = pe.matmul(ps, ones_r[:, :], bias_rows[:, :], start=False, stop=True)
                    if t % 2:
                        last.then_inc(v_ps, 1)

            def project_gate(i, blocks=range(KH)):
                for k in blocks:
                    if k == KH - 1 and follows_another(i):
                        pe.wait_ge(sim_biased, i + 1)
                    ps = bank[B_GATE[k]][:, :]
                    w = slice(WG + k * P, WG + (k + 1) * P)
                    pe.matmul(ps, att_hi[:, w], xt_hi[:, :], start=True, stop=False)
                    pe.matmul(ps, att_hi[:, w], xt_lo[:, :], start=False, stop=False)
                    pe.matmul(ps, att_lo[:, w], xt_hi[:, :], start=False, stop=True).then_inc(gate_ps, 1)

            def similarities(i):
                pe.wait_ge(quad_heads, i + 1)
                if not follows_another(i):
                    pe.wait_ge(gate_set, KH)
                for t in range(TILES):
                    last = pe.matmul(bank[B_SIM][:, cols(t)], head_t[:, QUAD_K, cols(t)],
                                     head_t[:, QUAD_Q, cols(t)], start=True, stop=True)
                last.then_inc(sim_ps, 1)

            def linear_scores(i):
                pe.wait_ge(lin_heads, i + 1)
                for t in range(TILES):
                    last = pe.matmul(bank[B_OTHER][:, cols(t)], head_t[:, LIN_K, cols(t)],
                                     head_t[:, LIN_Q, cols(t ^ 1)], start=True, stop=True)
                last.then_inc(other_ps, 1)
                for t in range(TILES):
                    last = pe.matmul(bank[same_bank(i)][:, cols(t)], head_t[:, LIN_K, cols(t)],
                                     head_t[:, LIN_Q, cols(t)], start=True, stop=True)
                last.then_inc(same_ps, 1)

            def mix(i, blocks=range(KH)):
                pe.wait_ge(v_set, 2 * i + 2)
                pe.wait_ge(other_set, i + 1)
                for k in blocks:
                    pe.wait_ge(gate_set, KH * i + k + 1)
                    for r in range(ROWS):
                        pe.wait_ge(same_set, ROWS * i + r + 1)
                        for t in range(2):
                            last = pe.matmul(bank[B_GATE[k]][:, r * ROW:(r + 1) * ROW],
                                             v_tok[:, 2 * r + t, k * P:(k + 1) * P],
                                             weights[:, r, 2 * t:2 * t + 2, :].rearrange("p a q -> p (a q)"),
                                             start=(t == 0), stop=(t == 1))
                    last.then_inc(mix_ps, 1)

            def project_out(i):
                pe.wait_ge(gated_set, KH * i + KH)
                for t in range(TILES):
                    for k in range(KH):
                        last = pe.matmul(bank[B_TOK][:, cols(t)], gated_t[:, k, cols(t)],
                                         att[:, WOUT + k * DIM:WOUT + (k + 1) * DIM],
                                         start=(k == 0), stop=(k == KH - 1))
                last.then_inc(proj_ps, 1)

            def turn_x1_hat(i):
                pe.wait_ge(x1_hat_set, i + 1)
                for t in range(TILES):
                    last = pe.transpose(bank[turn1_bank(i)][:, cols(t)], x1_hat[:, t, :], ident[:, :])
                last.then_inc(x1t_ps, 1)

            def weigh(ps, at, hi, lo, start, stop, with_lo):
                w = slice(at, at + P)
                pe.matmul(ps, ffn_hi[:, w], hi, start=start, stop=False)
                if with_lo:
                    pe.matmul(ps, ffn_lo[:, w], hi, start=False, stop=False)
                return pe.matmul(ps, ffn_hi[:, w], lo, start=False, stop=stop)

            def gated_layer(f, with_lo, part=WHOLE, blocks=range(KF)):
                s, tiles, b0 = part
                for m in blocks:
                    for at, b, done in ((W1, 2 * m % 4, w1_ps), (W2, 2 * m % 4 + 1, w2_ps)):
                        if m >= 2 and at == W1:
                            pe.wait_ge(silu_set, KF * f + m - 1)
                        if m >= 2 and at == W2:
                            pe.wait_ge(h0_set, KF * f + m - 1)
                        weigh(bank[b0 + b][:, s], at + m * P, x1t_hi[:, s], x1t_lo[:, s], True, True,
                              with_lo).then_inc(done, 1)

            def hidden_layer(f, at, hi, lo, hi_set, lo_set, done, blocks, with_lo, part):
                s, tiles, b0 = part

                def product(m, k):
                    return weigh(bank[b0 + m][:, s], at + k * FFN + m * P, hi[:, k, s], lo[:, k, s],
                                 k == 0, k == KF - 1, with_lo)

                early = [m for m in blocks if m < (2 if part is WHOLE else 1)]
                if early:
                    for k in range(KF - 1):
                        pe.wait_ge(hi_set, KF * f + k + 1)
                        pe.wait_ge(lo_set, KF * f + k + 1)
                        product(early[0], k)
                    for m in early[1:]:
                        for k in range(KF - 1):
                            product(m, k)
                    pe.wait_ge(hi_set, KF * f + KF)
                    pe.wait_ge(lo_set, KF * f + KF)
                    for m in early:
                        product(m, KF - 1).then_inc(done, 1)
                for m in blocks:
                    if m not in early:
                        for k in range(KF):
                            last = product(m, k)
                        last.then_inc(done, 1)

            def first_hidden_layer(f, with_lo, part=WHOLE, blocks=range(KF)):
                if 0 in blocks:
                    pe.wait_ge(silu_set, KF * f + KF)
                    pe.wait_ge(h0_set, KF * f + KF - 1)
                hidden_layer(f, H1, h0_hi, h0_lo, h0_hi_set, h0_lo_set, h1_ps, blocks, with_lo, part)

            def second_hidden_layer(f, with_lo, part=WHOLE, blocks=range(KF)):
                hidden_layer(f, H2, g1_hi, g1_lo, g1_hi_set, g1_lo_set, h2_ps, blocks, with_lo, part)

            def last_layer(f, blocks, with_lo, part=WHOLE):
                s, tiles, b0 = part
                for k in blocks:
                    pe.wait_ge(g2_hi_set, KF * f + k + 1)
                    pe.wait_ge(g2_lo_set, KF * f + k + 1)
                    last = weigh(bank[b0 + B_LAST][:, s], W3 + k * DIM, g2_hi[:, k, s], g2_lo[:, k, s],
                                 k == 0, k == KF - 1, with_lo)
                if KF - 1 in blocks:
                    last.then_inc(w3_ps, 1)

            def turn_z(f, tiles, to_bank):
                pe.wait_ge(z_set, f + 1)
                for t in tiles:
                    last = pe.transpose(bank[to_bank][:, cols(t)], z_t[:, cols(t)], ident[:, :])
                last.then_inc(z_tok_ps, 1)

            def keep_busy(products):
                for n in range(products):
                    pe.matmul(bank[B_SPARE][:, :], h0_hi[:, 0, 0:P], h0_hi[:, 0, :], start=True, stop=True)

            pe.wait_ge(consts_set, 1)
            keep_busy(WARM_UP)
            pe.wait_ge(rel_in, 48)
            pe.wait_ge(rel_wide_set, 1)
            for n in range(2):
                last = pe.matmul(bank[B_REL[n]][:, :], rel_wide[:, :], hot[:, n * CHUNK:(n + 1) * CHUNK],
                                 start=True, stop=True)
            last.then_inc(rel_ps, 1)
            pe.wait_ge(ident_in, 16)
            turn_x_hat(0)
            pe.wait_ge(att_in, 16)
            pe.wait_ge(lnb_set, 1)
            pe.matmul(bank[B_BIAS][0:BR, 0:HID], lnb_pair[:, :], att[:, WV:WV + HID],
                      start=True, stop=True).then_inc(bias_ps, 1)
            for k in range(KH + 1):
                last = pe.matmul(bank[B_BIAS][:, HID + k:HID + k + 1], att[:, WG + k * P:WG + (k + 1) * P],
                                 col(C_LNB), start=True, stop=True)
            last.then_inc(bias_ps, 1)
            keep_busy(KEEP_BUSY)
            pe.wait_ge(att_split, 1)
            project_qk(0)
            project_gate(0)
            pe.wait_ge(bias_split, 1)
            pe.wait_ge(gqk_set, 1)
            project_v(0)
            similarities(0)
            turn_x_hat(1)
            pe.wait_ge(rel_all_set, 1)
            linear_scores(0)
            pe.wait_ge(qk_set, 1)
            project_qk(1, bank_is_free=True)
            mix(0)
            project_v(1, range(TILES // 2))
            pe.wait_ge(out_w_in, 16)
            pe.wait_ge(qk_set, 2)
            project_out(0)
            project_v(1, range(TILES // 2, TILES))
            similarities(1)
            linear_scores(1)
            project_gate(1)
            mix(1)
            pe.wait_ge(lo_summed, len(FFN_PIECES))
            pe.matmul(bank[B_SPARE][0:1, 0:len(FFN_PIECES)], ones[:, :], lo_sums[:, :],
                      start=True, stop=True).then_inc(lo_ps, 1)
            turn_x1_hat(0)

            def steps(with_lo):
                def ffn_and_attention(i, ahead):
                    f = i - 1
                    pe.wait_ge(x1t_hi_set, f + 1)
                    pe.wait_ge(x1t_lo_set, f + 1)
                    gated_layer(f, with_lo)
                    project_out(i)
                    first_hidden_layer(f, with_lo, WHOLE, range(2))
                    if ahead:
                        turn_x_hat(i + 1)
                    first_hidden_layer(f, with_lo, WHOLE, range(2, KF))
                    if ahead:
                        pe.wait_ge(xt_hi_set, i + 2)
                        pe.wait_ge(xt_lo_set, i + 2)
                        project_gate(i + 1, [0])
                    second_hidden_layer(f, with_lo, WHOLE, range(KF - 1))
                    if not ahead:
                        turn_x1_hat(i)
                    second_hidden_layer(f, with_lo, WHOLE, [KF - 1])
                    if ahead:
                        project_qk(i + 1)
                    last_layer(f, range(KF - 1), with_lo)
                    if ahead:
                        project_v(i + 1, range(TILES // 2))
                        last_layer(f, [KF - 1], with_lo)
                        project_v(i + 1, range(TILES // 2, TILES))
                        pe.wait_ge(qk_set, i + 2)
                        turn_z(f, range(TILES), B_TOK)
                        similarities(i + 1)
                        linear_scores(i + 1)
                        project_gate(i + 1, [1])
                        turn_x1_hat(i)
                        mix(i + 1)

                with pe.Fori(1, CHUNKS - 1) as i:
                    ffn_and_attention(i, True)
                ffn_and_attention(CHUNKS - 1, False)
                (fa, a), (fb, b) = HALVES
                pe.wait_ge(x1t_hi_set, CHUNKS)
                pe.wait_ge(x1t_lo_set, CHUNKS)
                pe.wait_ge(y_att_set, CHUNKS)
                gated_layer(fa, with_lo, a, range(KF // 2))
                last_layer(CHUNKS - 2, [KF - 1], with_lo)
                gated_layer(fa, with_lo, a, range(KF // 2, KF))
                turn_z(CHUNKS - 2, range(TILES), B_LAST_Z)
                gated_layer(fb, with_lo, b, range(1))
                pe.wait_ge(z_copied, 1)
                gated_layer(fb, with_lo, b, range(1, 2))
                first_hidden_layer(fa, with_lo, a, range(KF // 2))
                gated_layer(fb, with_lo, b, range(2, KF))
                first_hidden_layer(fa, with_lo, a, range(KF // 2, KF))
                first_hidden_layer(fb, with_lo, b)
                second_hidden_layer(fa, with_lo, a)
                second_hidden_layer(fb, with_lo, b)
                last_layer(fa, range(KF), with_lo, a)
                last_layer(fb, range(KF), with_lo, b)
                for f, (s, tiles, b0) in HALVES:
                    turn_z(f, tiles, b0 + B_Z)

            pe.wait_ge(lo_flag_set, 1)
            has_lo = pe.value_load(lo_flag[0:1, 0:1], min_val=0, max_val=1)
            with pe.If(has_lo):
                steps(True)
            with pe.Else():
                steps(False)

        @block.scalar
        def _(act):
            def activations_qk(i):
                act.wait_ge(qk_ps, i + 1)
                act.activation(qk_t[:, :], bank[B_TOK][:, :], ACT.Silu,
                               bias=bias_gqk[:, KH:KH + 1]).then_inc(qk_set, 1)

            def activations_v(i):
                for n in range(2):
                    act.wait_ge(v_ps, 2 * i + n + 1)
                    act.activation(v_tok[:, 2 * n:2 * n + 2, :].rearrange("p t d -> p (t d)"),
                                   bank[B_V[n]][:, :], ACT.Silu).then_inc(v_set, 1)

            def activations_gate(i, blocks=range(KH)):
                for k in blocks:
                    act.wait_ge(gate_ps, KH * i + k + 1)
                    act.activation(gate_t[:, k, :], bank[B_GATE[k]][:, :], ACT.Silu,
                                   bias=bias_gqk[:, k:k + 1]).then_inc(gate_set, 1)

            def round_x_hat(i):
                act.wait_ge(xt_ps, i + 1)
                act.copy(xt_hi[:, :], bank[B_TURN][:, :]).then_inc(xt_hi_set, 1)

            def weigh_other_tile(i):
                act.wait_ge(other_ps, i + 1)
                act.mul(other_tile, bank[B_OTHER][:, :].rearrange("p (r t q) -> p r t q", r=ROWS, t=2),
                        1.0 / ROW).then_inc(other_set, 1)

            def round_ffn(p):
                a, b = FFN_PIECES[p]
                act.wait_ge(ffn_in[p], 16)
                act.copy(ffn_hi[:, a:b], ffn[:, a:b]).then_inc(ffn_rounded, 1)

            def sum_ffn_low(p):
                a, b = FFN_PIECES[p]
                act.wait_ge(ffn_split[p], 1)
                act.activation(ffn[:, a:b], ffn_lo[:, a:b].bitcast(F32), ACT.Abs,
                               accum_out=lo_sums[:, p:p + 1]).then_inc(lo_summed, 1)

            def round_x1_hat(i):
                act.wait_ge(x1t_ps, i + 1)
                act.copy(x1t_hi[:, :], bank[turn1_bank(i)][:, :]).then_inc(x1t_hi_set, 1)

            def silu_w1(f, part=WHOLE, blocks=range(KF)):
                s, tiles, b0 = part
                for m in blocks:
                    act.wait_ge(w1_ps, KF * f + m + 1)
                    act.activation(silu_t[:, m, s], bank[b0 + 2 * m % 4][:, s], ACT.Silu,
                                   scale=col(C_S1 + m)).then_inc(silu_set, 1)

            def gelus(f, ps_done, scale, hi, hi_set, part=WHOLE, blocks=range(KF)):
                s, tiles, b0 = part
                for m in blocks:
                    act.wait_ge(ps_done, KF * f + m + 1)
                    act.activation(gelu_t[:, m, s], bank[b0 + m][:, s], ACT.Gelu,
                                   scale=col(scale + m))
                    act.activation(hi[:, m, s], bank[b0 + m][:, s], ACT.Gelu,
                                   scale=col(scale + m)).then_inc(hi_set, 1)

            def scale_z(f, part=WHOLE):
                s, tiles, b0 = part
                act.wait_ge(w3_ps, f + 1)
                act.mul(z_t[:, s], bank[b0 + B_LAST][:, s], col(C_S3)).then_inc(z_set, 1)

            act.dma_start(rel[:, :], rel_emb).then_inc(rel_in, 16)
            act.dma_start(hot[:, :], one_hot).then_inc(rel_in, 16)
            act.dma_start(own_key[:, :], own_keys).then_inc(rel_in, 16)
            act.wait_ge(consts_set, 1)
            act.activation(unused[:, :], ones[:, :], ACT.Silu)
            for row in (0, GROUP):
                act.dma_start(bias_raw[row:row + 1, :], bias_v).then_inc(bias_in, 16)
            act.dma_start(bout[:, :], b_out.partition_broadcast(P)).then_inc(bout_in, 16)

            act.wait_ge(att_scaled, 1)
            act.copy(att_hi[:, :], att_g).then_inc(att_rounded, 1)
            round_x_hat(0)
            act.wait_ge(rel_ps, 1)
            for n in range(2):
                last = act.copy(silu_h0[:, 2 + n, :], bank[B_REL[n]][:, :])
            last.then_inc(rel_all_set, 1)
            round_ffn(0)
            act.wait_ge(gqk_set, 1)
            activations_qk(0)
            activations_gate(0)
            activations_v(0)
            round_x_hat(1)
            weigh_other_tile(0)
            round_ffn(1)
            act.wait_ge(lin_heads, 1)
            act.wait_ge(quad_heads, 1)
            activations_qk(1)
            round_ffn(2)
            for p in range(3, len(FFN_PIECES)):
                round_ffn(p)
            sum_ffn_low(0)
            sum_ffn_low(1)
            activations_v(1)
            weigh_other_tile(1)
            activations_gate(1)
            sum_ffn_low(2)
            for p in range(3, len(FFN_PIECES)):
                sum_ffn_low(p)
            round_x1_hat(0)

            def step(i, ahead):
                silu_w1(i - 1)
                gelus(i - 1, h1_ps, C_SH1, g1_hi, g1_hi_set, blocks=range(2))
                if ahead:
                    round_x_hat(i + 1)
                gelus(i - 1, h1_ps, C_SH1, g1_hi, g1_hi_set, blocks=range(2, KF))
                gelus(i - 1, h2_ps, C_SH2, g2_hi, g2_hi_set, blocks=range(KF - 1))
                if not ahead:
                    round_x1_hat(i)
                gelus(i - 1, h2_ps, C_SH2, g2_hi, g2_hi_set, blocks=[KF - 1])
                if ahead:
                    activations_qk(i + 1)
                    scale_z(i - 1)
                    activations_v(i + 1)
                    activations_gate(i + 1, [0])
                    weigh_other_tile(i + 1)
                    activations_gate(i + 1, [1])
                    round_x1_hat(i)

            with act.Fori(1, CHUNKS - 1) as i:
                step(i, True)
            step(CHUNKS - 1, False)
            (fa, a), (fb, b) = HALVES
            silu_w1(fa, a, range(KF // 2))
            scale_z(CHUNKS - 2)
            silu_w1(fa, a, range(KF // 2, KF))
            act.wait_ge(z_tok_ps, CHUNKS - 1)
            act.copy(flat(z_tok), bank[B_LAST_Z][:, :]).then_inc(z_copied, 1)
            silu_w1(fb, b)
            for f, part in HALVES:
                gelus(f, h1_ps, C_SH1, g1_hi, g1_hi_set, part)
            for f, part in HALVES:
                gelus(f, h2_ps, C_SH2, g2_hi, g2_hi_set, part)
            for f, part in HALVES:
                scale_z(f, part)

        @block.vector
        def _(dve):
            def statistics(name, i, tile_of, tiles=range(TILES)):
                for t in tiles:
                    last = dve.bn_stats(bn[name][:, t, :], tile_of(t))
                last.then_inc(bn_done[name], 1)
                dve.wait_ge(bn_done[name], i + 1)
                dve.sem_inc(waits_passed, 1)
                for t in tiles:
                    last = dve.bn_aggr(mv[name][:, t, :], bn[name][:, t, :])
                last.then_inc(mv_done[name], 1)

            def normalize(name, to, tile_of, done, root=0, tiles=range(TILES)):
                for t in tiles:
                    last = dve.tensor_scalar(to[:, t, :], tile_of(t), mv[name][:, t, 0:1],
                                             rstd[name][:, root + t:root + t + 1],
                                             ALU.subtract, ALU.mult)
                last.then_inc(done, 1)

            def of(buffer):
                return lambda t: buffer[:, t, :]

            def of_bank(b):
                return lambda t: bank[b][:, cols(t)]

            def x_statistics(i):
                name, n, source = x_norm_of(i)
                if follows_another(i):
                    dve.wait_ge(x_loaded, 16 * i)
                else:
                    dve.wait_ge(res_loaded, 16)
                statistics(name, n, of(source))

            def x_normalize_twice(i):
                name, n, source = x_norm_of(i)
                dve.wait_ge(rstd_done[name], n + 1)
                normalize(name, x_hat, of(source), x_hat_set, root=TILES)

            def x_normalize(i):
                name, n, source = x_norm_of(i)
                if follows_another(i):
                    dve.wait_ge(norm_b_set, i)
                else:
                    dve.wait_ge(rstd_done[name], 2)
                normalize(name, x_norm, of(source), x_normed)

            def low_x_hat(i):
                dve.wait_ge(xt_hi_set, i + 1)
                dve.tensor_tensor(xt_lo[:, :], bank[B_TURN][:, :], xt_hi[:, :].bitcast(F32),
                                  ALU.subtract).then_inc(xt_lo_set, 1)

            def quadratic_heads(i):
                dve.wait_ge(qk_set, i + 1)
                for h in (QUAD_K, QUAD_Q):
                    last = dve.tensor_scalar(head_t[:, h, :], qk_t[:, :], col(C_GAMMA + h),
                                             col(C_BETA + h), ALU.mult, ALU.add)
                last.then_inc(quad_heads, 1)

            def bias_similarities(i):
                dve.wait_ge(sim_ps, i + 1)
                dve.scalar_tensor_tensor(sim_b[:, :, :], bank[B_SIM][:, :].rearrange("p (t q) -> p t q", q=P),
                                         1.0 / GROUP, rel_bias[:, :].unsqueeze(1).broadcast_to([P, TILES, P]),
                                         ALU.mult, ALU.add).then_inc(sim_biased, 1)

            def square_relu(i):
                dve.wait_ge(sim_biased, i + 1)
                dve.scalar_tensor_tensor(flat(attn), flat(sim_b), 0.0, flat(sim_b),
                                         ALU.max, ALU.mult).then_inc(attn_set, 1)

            def weigh_same_tile(i):
                dve.wait_ge(same_ps, i + 1)
                dve.wait_ge(attn_set, i + 1)
                for r in range(ROWS):
                    dve.scalar_tensor_tensor(
                        same_tile[:, r, :, :],
                        bank[same_bank(i)][:, r * ROW:(r + 1) * ROW].rearrange("p (t q) -> p t q", q=P),
                        1.0 / ROW, attn[:, 2 * r:2 * r + 2, :], ALU.mult, ALU.add).then_inc(same_set, 1)

            def gate_mix(i):
                for k in range(KH):
                    dve.wait_ge(mix_ps, KH * i + k + 1)
                    dve.tensor_tensor(gated_t[:, k, :], bank[B_GATE[k]][:, :], gate_t[:, k, :],
                                      ALU.mult).then_inc(gated_set, 1)

            def add_x_norm(i):
                dve.wait_ge(proj_ps, i + 1)
                dve.wait_ge(norm_b_set, i + 1)
                dve.tensor_tensor(flat(y_att), bank[B_TOK][:, :], flat(x_norm_b),
                                  ALU.add).then_inc(y_att_set, 1)
                dve.wait_ge(y_att_set, i + 1)
                statistics("att", i, of(y_att))

            def y_normalize(i):
                dve.wait_ge(rstd_done["att"], i + 1)
                normalize("att", y_hat, of(y_att), y_hat_set)

            def add_x(i):
                dve.wait_ge(y_hat_set, i + 1)
                dve.wait_ge(res_loaded, 16 * i + 16)
                if follows_another(i):
                    dve.wait_ge(x1_kept, i)
                dve.tensor_tensor(flat(x1), flat(y_hat), flat(x_res), ALU.add).then_inc(x1_set, 1)

            def x1_statistics(i):
                dve.wait_ge(x1_set, i + 1)
                statistics("x1", i, of(x1))

            def x1_normalize(i):
                dve.wait_ge(rstd_done["x1"], i + 1)
                normalize("x1", x1_hat, of(x1), x1_hat_set)

            def low_x1_hat(i):
                dve.wait_ge(x1t_hi_set, i + 1)
                dve.tensor_tensor(x1t_lo[:, :], bank[turn1_bank(i)][:, :], x1t_hi[:, :].bitcast(F32),
                                  ALU.subtract).then_inc(x1t_lo_set, 1)

            def gated_product(f, m, part=WHOLE):
                s, tiles, b0 = part
                dve.wait_ge(silu_set, KF * f + m + 1)
                dve.wait_ge(w2_ps, KF * f + m + 1)
                dve.scalar_tensor_tensor(h0[:, m, s], bank[b0 + 2 * m % 4 + 1][:, s], col(C_S2 + m),
                                         silu_t[:, m, s], ALU.mult, ALU.mult).then_inc(h0_set, 1)

            def low_h0(f, m, part=WHOLE):
                s, tiles, b0 = part
                dve.wait_ge(h0_hi_set, KF * f + m + 1)
                dve.tensor_tensor(h0_lo[:, m, s], h0[:, m, s], h0_hi[:, m, s].bitcast(F32),
                                  ALU.subtract).then_inc(h0_lo_set, 1)

            def gated_layer(f, part=WHOLE, first_is_made=False):
                if not first_is_made:
                    gated_product(f, 0, part)
                for m in range(1, KF):
                    gated_product(f, m, part)
                    low_h0(f, m - 1, part)
                low_h0(f, KF - 1, part)

            def low_gelu(f, m, hi, lo, hi_set, lo_set, part=WHOLE):
                s, tiles, b0 = part
                dve.wait_ge(hi_set, KF * f + m + 1)
                dve.tensor_tensor(lo[:, m, s], gelu_t[:, m, s], hi[:, m, s].bitcast(F32),
                                  ALU.subtract).then_inc(lo_set, 1)

            def z_statistics(f, b=B_TOK, tiles=range(TILES)):
                dve.wait_ge(z_tok_ps, f + 1)
                statistics("ffn", f, of_bank(b), tiles)

            def z_normalize(f, b=B_TOK, tiles=range(TILES)):
                dve.wait_ge(rstd_done["ffn"], f + 1)
                normalize("ffn", z_hat, of_bank(b), z_hat_set, tiles=tiles)

            dve.memset(h0_hi[:, 0, :].bitcast(F32), 1.0)
            dve.memset(minus_half[:, :], -0.5)
            dve.memset(ones[:, :], 1.0)
            dve.memset(ones_r[:, :].bitcast(F32), 1.0)
            dve.memset(lnb_pair[:, :], 0.0)
            dve.memset(rel_bias[:, :], MASKED)
            dve.memset(bias_raw[:, :], 0.0).then_inc(consts_set, 1)
            x_statistics(0)
            dve.wait_ge(consts_set, 1)
            dve.wait_ge(vec_in, 16)
            for c in (0, GROUP):
                last = dve.tensor_copy(lnb_pair[:, c:c + 1], col(C_LNB))
            last.then_inc(lnb_set, 1)
            dve.wait_ge(rel_in, 48)
            dve.tensor_scalar(rel_wide[:, :], rel[:, 0:1].broadcast_to([BUCKETS, P]), 1.0, None,
                              ALU.mult).then_inc(rel_wide_set, 1)
            dve.wait_ge(att_in, 16)
            dve.tensor_scalar(att_g, att[:, 0:WOUT], col(C_LNG), None, ALU.mult).then_inc(att_scaled, 1)
            x_normalize_twice(0)
            x_statistics(1)
            dve.wait_ge(att_rounded, 1)
            dve.tensor_tensor(att_lo[:, :], att_g, att_hi[:, :].bitcast(F32),
                              ALU.subtract).then_inc(att_split, 1)
            low_x_hat(0)
            dve.wait_ge(bias_ps, 2)
            dve.wait_ge(bias_in, 32)
            dve.tensor_tensor(bias_gqk[:, :], bank[B_BIAS][:, HID:HID + KH + 1], col(C_BG, KH + 1),
                              ALU.add).then_inc(gqk_set, 1)
            dve.tensor_tensor(bias_sum[:, :], bank[B_BIAS][0:BR, 0:HID], bias_raw[:, :],
                              ALU.add).then_inc(bias_added, 1)
            dve.wait_ge(bias_added, 1)
            dve.tensor_copy(bias_rnd[:, :], bias_sum[:, :])
            dve.tensor_copy(bias_rows[:, :], bias_sum[:, :]).then_inc(bias_added, 1)
            dve.wait_ge(bias_added, 2)
            dve.tensor_tensor(bias_rows[GROUP:BR, :], bias_sum[GROUP:BR, :],
                              bias_rnd[GROUP:BR, :].bitcast(F32), ALU.subtract).then_inc(bias_split, 1)
            quadratic_heads(0)
            x_normalize_twice(1)
            dve.wait_ge(rel_set, 1)
            dve.reduce_sum(rel_group[:, :], rel_picked, AX_X).then_inc(rel_set, 1)
            dve.wait_ge(rel_set, 2)
            for g in range(P // GROUP):
                s = slice(g * GROUP, (g + 1) * GROUP)
                last = dve.tensor_scalar(rel_bias[s, s], rel_group[s, :], float(DIM) ** 0.5, None, ALU.mult)
            last.then_inc(rel_set, 1)
            dve.wait_ge(rel_set, 3)
            bias_similarities(0)
            low_x_hat(1)
            square_relu(0)
            weigh_same_tile(0)
            x_normalize(0)
            quadratic_heads(1)
            gate_mix(0)
            for p in range(PIECES_OF_POOL, len(FFN_PIECES)):
                a, b = FFN_PIECES[p]
                dve.wait_ge(ffn_rounded, p + 1)
                dve.tensor_tensor(ffn_lo[:, a:b], ffn[:, a:b], ffn_hi[:, a:b].bitcast(F32),
                                  ALU.subtract).then_inc(ffn_split[p], 1)
            add_x_norm(0)
            bias_similarities(1)
            square_relu(1)
            y_normalize(0)
            add_x(0)
            weigh_same_tile(1)
            x1_statistics(0)
            x_normalize(1)
            x1_normalize(0)
            dve.wait_ge(lo_ps, 1)
            dve.reduce_sum(lo_total[:, :], bank[B_SPARE][0:1, 0:len(FFN_PIECES)], AX_X).then_inc(lo_total_set, 1)
            dve.wait_ge(lo_total_set, 1)
            dve.tensor_scalar(lo_flag[:, :], lo_total[:, :], 0.0, None, ALU.is_gt).then_inc(lo_flag_set, 1)
            low_x1_hat(0)

            def low_gelu1(f, m):
                low_gelu(f, m, g1_hi, g1_lo, g1_hi_set, g1_lo_set)

            def low_gelu2(f, m):
                low_gelu(f, m, g2_hi, g2_lo, g2_hi_set, g2_lo_set)

            def step(i, ahead):
                f = i - 1
                if ahead:
                    x_statistics(i + 1)
                gate_mix(i)
                gated_layer(f)
                if ahead:
                    x_normalize_twice(i + 1)
                add_x_norm(i)
                low_gelu1(f, 0)
                low_gelu1(f, 1)
                if ahead:
                    low_x_hat(i + 1)
                y_normalize(i)
                low_gelu1(f, 2)
                add_x(i)
                low_gelu1(f, 3)
                x1_statistics(i)
                if ahead:
                    x_normalize(i + 1)
                    low_gelu2(f, 0)
                    low_gelu2(f, 1)
                    x1_normalize(i)
                else:
                    x1_normalize(i)
                    low_gelu2(f, 0)
                    low_gelu2(f, 1)
                low_gelu2(f, 2)
                if not ahead:
                    low_x1_hat(i)
                low_gelu2(f, 3)
                if ahead:
                    quadratic_heads(i + 1)
                    z_statistics(f)
                    bias_similarities(i + 1)
                    square_relu(i + 1)
                    weigh_same_tile(i + 1)
                    z_normalize(f)
                    low_x1_hat(i)

            with dve.Fori(1, CHUNKS - 1) as i:
                step(i, True)
            step(CHUNKS - 1, False)
            (fa, a), (fb, b) = HALVES
            gated_layer(fa, a)
            gated_product(fb, 0, b)
            dve.wait_ge(z_copied, 1)
            statistics("ffn", CHUNKS - 2, of(z_tok))
            gated_layer(fb, b, first_is_made=True)
            dve.wait_ge(rstd_done["ffn"], CHUNKS - 1)
            normalize("ffn", z_hat, of(z_tok), z_hat_set)
            for f, part in HALVES:
                for m in range(KF):
                    low_gelu(f, m, g1_hi, g1_lo, g1_hi_set, g1_lo_set, part)
            for f, part in HALVES:
                for m in range(KF):
                    low_gelu(f, m, g2_hi, g2_lo, g2_hi_set, g2_lo_set, part)
            for f, (s, tiles, b0) in HALVES:
                z_statistics(f, b0 + B_Z, tiles)
            for f, (s, tiles, b0) in HALVES:
                z_normalize(f, b0 + B_Z, tiles)
                dve.wait_ge(z_hat_set, f + 1)
                dve.wait_ge(out_free, 16 * CHUNKS)
                dve.wait_ge(x1_kept, CHUNKS)
                a, b = tiles[0], tiles[-1] + 1
                dve.tensor_tensor(y_out[:, a:b, :], z_hat[:, a:b, :], x1_res[:, a:b, :],
                                  ALU.add).then_inc(out_ready, 1)

        @block.gpsimd
        def _(pool):
            def after(semaphore, value):
                pool.wait_ge(semaphore, value)
                pool.sem_inc(waits_passed, 1)

            def root(name, i, tiles=range(TILES), once=True, twice=False):
                after(mv_done[name], 1 if name == "x0" else i + 1)
                a, b = tiles[0], tiles[-1] + 1
                if once:
                    last = pool.tensor_scalar(arg[name][:, a:b], mv[name][:, a:b, 1], 1.0, EPS,
                                              ALU.mult, ALU.add)
                if twice:
                    last = pool.tensor_scalar(arg[name][:, TILES:2 * TILES], mv[name][:, :, 1], 1.0 + EPS,
                                              EPS * EPS, ALU.mult, ALU.add)
                    a, b = (a if once else TILES), 2 * TILES
                last.then_inc(arg_done[name], 1)
                pool.wait_ge(arg_done[name], i + 1)
                pool.tensor_tensor(rstd[name][:, a:b], arg[name][:, a:b], minus_half[:, a:b],
                                   ALU.pow).then_inc(rstd_done[name], 1)

            def root_x(i):
                name, n, source = x_norm_of(i)
                if follows_another(i):
                    root(name, n, twice=True)
                else:
                    root(name, 0, once=False, twice=True)

            def add_b_out(i):
                pool.wait_ge(x_normed, i + 1)
                if follows_another(i):
                    pool.wait_ge(y_att_set, i)
                pool.tensor_tensor(x_norm_b[:, :, :], x_norm[:, :, :],
                                   bout[:, :].unsqueeze(1).broadcast_to([P, TILES, DIM]),
                                   ALU.add).then_inc(norm_b_set, 1)

            def linear_heads(i):
                after(qk_set, i + 1)
                for h in (LIN_Q, LIN_K):
                    last = pool.tensor_scalar(head_t[:, h, :], qk_t[:, :], col(C_GAMMA + h),
                                              col(C_BETA + h), ALU.mult, ALU.add)
                last.then_inc(lin_heads, 1)

            def round_h0(f, part=WHOLE):
                s, tiles, b0 = part
                for m in range(KF):
                    after(h0_set, KF * f + m + 1)
                    pool.tensor_scalar(h0_hi[:, m, s], h0[:, m, s], 1.0, 0.0,
                                       ALU.mult, ALU.add).then_inc(h0_hi_set, 1)

            def keep_x1(f):
                if follows_another(f):
                    pool.wait_ge(out_ready, f)
                after(x1_set, f + 1)
                pool.tensor_scalar(flat(x1_res), flat(x1), 1.0, 0.0, ALU.mult, ALU.add).then_inc(x1_kept, 1)

            def make_out(f):
                pool.wait_ge(z_hat_set, f + 1)
                pool.wait_ge(out_free, 16 * f + 16)
                pool.tensor_tensor(flat(y_out), flat(z_hat), flat(x1_res), ALU.add).then_inc(out_ready, 1)

            pool.wait_ge(consts_set, 1)
            root_x(0)
            root_x(1)
            pool.wait_ge(rel_all_set, 1)
            pool.tensor_tensor(rel_picked, rel_all, own_key[:, :].unsqueeze(1).broadcast_to([P, GROUP, GROUP]),
                               ALU.mult).then_inc(rel_set, 1)
            pool.wait_ge(vec_in, 16)
            pool.wait_ge(bout_in, 16)
            linear_heads(0)
            root("x0", 1)

            def low_ffn(p):
                a, b = FFN_PIECES[p]
                pool.wait_ge(ffn_rounded, p + 1)
                pool.tensor_tensor(ffn_lo[:, a:b], ffn[:, a:b], ffn_hi[:, a:b].bitcast(F32),
                                   ALU.subtract).then_inc(ffn_split[p], 1)

            low_ffn(0)
            low_ffn(1)
            low_ffn(2)
            add_b_out(0)
            pool.wait_ge(same_ps, 1)
            linear_heads(1)
            root("att", 0)
            low_ffn(3)
            root("x1", 0)
            keep_x1(0)
            add_b_out(1)

            def step(i, ahead):
                if ahead:
                    root_x(i + 1)
                round_h0(i - 1)
                root("att", i)
                root("x1", i)
                if ahead:
                    add_b_out(i + 1)
                    linear_heads(i + 1)
                    root("ffn", i - 1)
                    make_out(i - 1)
                    keep_x1(i)

            with pool.Fori(1, CHUNKS - 1) as i:
                step(i, True)
            step(CHUNKS - 1, False)
            (fa, a), (fb, b) = HALVES
            round_h0(fa, a)
            round_h0(fb, b)
            root("ffn", CHUNKS - 2)
            make_out(CHUNKS - 2)
            keep_x1(CHUNKS - 1)
            for f, (s, tiles, b0) in HALVES:
                root("ffn", f, tiles=tiles)


def _bucket_table():
    pos = np.arange(GROUP)
    n = -(pos[None, :] - pos[:, None])
    nb = BUCKETS // 2
    ret = (n < 0).astype(np.int32) * nb
    n = np.abs(n)
    exact = nb // 2
    ratio = np.log(np.maximum(n, 1).astype(np.float32) / np.float32(exact)) / np.float32(np.log(MAX_DIST / exact))
    large = exact + (ratio * np.float32(nb - exact)).astype(np.int32)
    return ret + np.where(n < exact, n, np.minimum(large, nb - 1))


def _one_hot():
    hot = _bucket_table()[None, :, :] == np.arange(BUCKETS)[:, None, None]
    return hot.reshape(BUCKETS, -1).astype(np.float32)


def _blocks(w):
    o, n = w.shape
    return w.T.reshape(n // P, P, o).transpose(1, 0, 2).reshape(P, -1)


def _columns(v):
    return v.reshape(-1, P).T


def kernel(**inputs):
    import concourse.bacc as _bacc
    from concourse.bass_utils import run_bass_kernel_spmd as _run

    a = {k.removeprefix("L0_"): np.asarray(v) for k, v in inputs.items()}
    w_h, b_h = a["attn_W_h"], a["attn_b_h"]
    w_out = a["attn_W_out"].reshape(KH, P, DIM).transpose(1, 0, 2).reshape(P, -1)
    layout = {
        "x": a["attn_x"].reshape(TOKENS, DIM),
        "att_w": np.concatenate([w_h, a["attn_W_qk"], w_out], axis=1),
        "ffn_w": np.concatenate([_blocks(a[f"ffn_{n}_w"]) for n in ("w1", "w2", "h1", "h2", "w3")], axis=1),
        "vectors": np.concatenate(
            [_columns(v) for v in (a["attn_ln_g"], a["attn_ln_b"], b_h[HID:], a["attn_b_qk"],
                                   a["attn_os_gamma"], a["attn_os_beta"], a["ffn_w1_s"], a["ffn_w2_s"],
                                   a["ffn_h1_s"], a["ffn_h2_s"], a["ffn_w3_s"])], axis=1),
        "bias_v": b_h[:HID].reshape(1, HID),
        "b_out": a["attn_b_out"].reshape(1, DIM),
        "rel_emb": a["attn_rel_emb"],
        "one_hot": _one_hot(),
        "own_keys": np.tile(np.eye(GROUP, dtype=np.float32), (P // GROUP, 1)),
        "identity": np.eye(P, dtype=np.float32),
    }
    nc = _bacc.Bacc("TRN2", target_bir_lowering=False, num_devices=1)
    arrays, args = {}, []
    for name, v in layout.items():
        v = np.ascontiguousarray(v)
        arrays[f"in_{name}"] = v
        args.append(nc.dram_tensor(f"in_{name}", v.shape, F32, kind="ExternalInput").ap())
    out = nc.dram_tensor("out_x", (TOKENS, DIM), F32, kind="ExternalOutput").ap()
    build(nc, *args, out)
    r = _run(nc, [arrays], core_ids=[0])
    return r.results[0]["out_x"].reshape(inputs["L0_attn_x"].shape)
```
